# Optimizing a Trainium2 kernel written in Bass

```python
import numpy as np
import jax
import jax.numpy as jnp

def _softmax(x, axis=-1):
    return jax.nn.softmax(x, axis=axis)

def _gelu(x):
    return jax.nn.gelu(x, approximate=True)

def _silu(x):
    return jax.nn.silu(x)

def _sigmoid(x):
    return jax.nn.sigmoid(x)

def _layernorm(x, axis=-1, eps=1e-05):
    m = jnp.mean(x, axis=axis, keepdims=True)
    v = jnp.var(x, axis=axis, keepdims=True)
    return (x - m) / jnp.sqrt(v + eps)

def _scatter_add(tgt, idx, src, axis=0):
    return tgt.at[idx].add(src)

def _segment_sum(src, seg, n):
    return jax.ops.segment_sum(src, seg, n)
kernel_name = 'mk_lm_tower_d1_tok_ids4096_r4_63a217'

def setup_inputs(seed: int=0):
    np.random.seed(seed)
    _w = jnp.asarray

    def _rec_inputs():
        import jax
        import jax.numpy as jnp
        _rk = jax.random.key(seed)
        x = jax.random.randint(jax.random.fold_in(_rk, 1), (8, 512), 0, 8192, jnp.int32)
        return x
    x = _rec_inputs()

    def _L0_tok_setup():
        import jax, jax.numpy as jnp
        import numpy as np
        ORIG_VOCAB = 8000
        key = jax.random.key(seed)
        k1, k2, k3 = jax.random.split(key, 3)
        x = jax.random.randint(k1, (8, 1024), 0, 8192, dtype=jnp.int64)
        orig_emb_w = jax.random.normal(k2, (8000, 1024), dtype=jnp.float32)
        new_emb = jax.random.normal(k3, (192, 1024), dtype=jnp.float32)
        return {'x': x, 'orig_emb_w': orig_emb_w, 'new_emb': new_emb}
    _L0_tok_all = _L0_tok_setup()
    _L0_tok_in = {k: v for k, v in _L0_tok_all.items() if k in ('orig_emb_w', 'new_emb')}
    del _L0_tok_all

    def _L0_attn_setup():
        import jax, jax.numpy as jnp
        import numpy as np
        N_STATE = 64
        SEQ_L = 1024
        BATCH, HCH = (16, 128)
        DT_MIN, DT_MAX = (0.001, 0.1)

        def _make_DPLR_HiPPO(N):
            P = np.sqrt(1 + 2 * np.arange(N))
            A = P[:, None] * P[None, :]
            A = np.tril(A) - np.diag(np.arange(N))
            nhippo = -A
            p = 0.5 * np.sqrt(2 * np.arange(1, N + 1) + 1.0)
            q = 2 * p
            S = nhippo + p[:, None] * q[None, :]
            Lambda, V = np.linalg.eig(S)
            Vc = V.conj().T
            p_t = Vc @ p
            q_t = Vc @ q.conj()
            return (Lambda, p_t, q_t, Vc)

        def _ri(z):
            return np.stack([z.real, z.imag], axis=-1).astype(np.float32)

        def _cplx(x_ri):
            return x_ri[..., 0] + 1j * x_ri[..., 1]

        def _s4_kernel(Lambda, p, q, B, Ct, step, L):
            Omega = jnp.exp(-2j * jnp.pi * (jnp.arange(L) / L))
            g = 2.0 / step * ((1.0 - Omega) / (1.0 + Omega))
            c = 2.0 / (1.0 + Omega)
            denom = g[:, None] - Lambda[None, :]
            cauchy = lambda v: (v[None, :] / denom).sum(-1)
            k00 = cauchy(Ct.conj() * B)
            k01 = cauchy(Ct.conj() * p)
            k10 = cauchy(q.conj() * B)
            k11 = cauchy(q.conj() * p)
            at_roots = c * (k00 - k01 * (1.0 / (1.0 + k11)) * k10)
            return jnp.fft.ifft(at_roots, L).real
        key = jax.random.key(seed)
        k_u, k_ct, k_b, k_d, k_ls = jax.random.split(key, 5)
        Lambda, p, q, Vc = _make_DPLR_HiPPO(N_STATE)
        u = jax.random.normal(k_u, (BATCH, HCH, SEQ_L), dtype=jnp.float32)
        Ct_ri = jax.random.normal(k_ct, (1, N_STATE, 2), dtype=jnp.float32) / np.sqrt(N_STATE)
        Bp = jax.random.normal(k_b, (N_STATE, 1), dtype=jnp.float32) / np.sqrt(N_STATE)
        D = jax.random.uniform(k_d, (1,), dtype=jnp.float32)
        log_step = jax.random.uniform(k_ls, (1,), dtype=jnp.float32, minval=np.log(DT_MIN), maxval=np.log(DT_MAX))
        return {'u': u, 'Lambda_ri': jnp.asarray(_ri(Lambda)), 'p_ri': jnp.asarray(_ri(p)), 'q_ri': jnp.asarray(_ri(q)), 'Vc_ri': jnp.asarray(_ri(Vc)), 'Ct_ri': Ct_ri, 'Bp': Bp, 'D': D, 'log_step': log_step}
    _L0_attn_all = _L0_attn_setup()
    _L0_attn_in = {k: v for k, v in _L0_attn_all.items() if k in ('Lambda_ri', 'p_ri', 'q_ri', 'Vc_ri', 'Ct_ri', 'Bp', 'D', 'log_step')}
    del _L0_attn_all

    def _L0_ffn_setup():
        import jax, jax.numpy as jnp
        import numpy as np
        R = 16
        LORA_ALPHA = 16
        SCALING = LORA_ALPHA / R
        key = jax.random.key(seed)
        kx, kr, ka = jax.random.split(key, 3)
        B, S, D, DO, E = (4, 512, 1024, 1024, 8)
        x = jax.random.normal(kx, (B, S, D), dtype=jnp.float32)
        bound_r = 1.0 / np.sqrt(D)
        route_w = jax.random.uniform(kr, (E, D), jnp.float32, -bound_r, bound_r)
        bound_a = 1.0 / np.sqrt(D)
        A = jax.random.uniform(ka, (E, R, D), jnp.float32, -bound_a, bound_a)
        kb = jax.random.fold_in(key, 7)
        Bw = jax.random.normal(kb, (E, DO, R), dtype=jnp.float32) * 0.02
        return {'x': x, 'route_w': route_w, 'A': A, 'Bw': Bw}
    _L0_ffn_all = _L0_ffn_setup()
    _L0_ffn_in = {k: v for k, v in _L0_ffn_all.items() if k in ('route_w', 'A', 'Bw')}
    del _L0_ffn_all
    return {'x': x, 'L0_tok_orig_emb_w': _L0_tok_in['orig_emb_w'], 'L0_tok_new_emb': _L0_tok_in['new_emb'], 'L0_attn_Lambda_ri': _L0_attn_in['Lambda_ri'], 'L0_attn_p_ri': _L0_attn_in['p_ri'], 'L0_attn_q_ri': _L0_attn_in['q_ri'], 'L0_attn_Vc_ri': _L0_attn_in['Vc_ri'], 'L0_attn_Ct_ri': _L0_attn_in['Ct_ri'], 'L0_attn_Bp': _L0_attn_in['Bp'], 'L0_attn_D': _L0_attn_in['D'], 'L0_attn_log_step': _L0_attn_in['log_step'], 'L0_ffn_route_w': _L0_ffn_in['route_w'], 'L0_ffn_A': _L0_ffn_in['A'], 'L0_ffn_Bw': _L0_ffn_in['Bw']}

def reference(x, L0_tok_orig_emb_w, L0_tok_new_emb, L0_attn_Lambda_ri, L0_attn_p_ri, L0_attn_q_ri, L0_attn_Vc_ri, L0_attn_Ct_ri, L0_attn_Bp, L0_attn_D, L0_attn_log_step, L0_ffn_route_w, L0_ffn_A, L0_ffn_Bw):
    import jax
    import jax.numpy as jnp

    def _L0_tok_ref(x, orig_emb_w, new_emb):
        import jax, jax.numpy as jnp
        import numpy as np
        ORIG_VOCAB = 8000
        x = x.astype(jnp.int32)
        is_new = x >= ORIG_VOCAB
        idx_new = jnp.clip(x - ORIG_VOCAB, 0, new_emb.shape[0] - 1)
        idx_old = jnp.clip(x, 0, orig_emb_w.shape[0] - 1)
        e_new = new_emb[idx_new]
        e_old = orig_emb_w[idx_old]
        return jnp.where(is_new[..., None], e_new, e_old)

    def _L0_attn_ref(u, Lambda_ri, p_ri, q_ri, Vc_ri, Ct_ri, Bp, D, log_step):
        import jax, jax.numpy as jnp
        import numpy as np
        N_STATE = 64
        SEQ_L = 1024
        BATCH, HCH = (16, 128)
        DT_MIN, DT_MAX = (0.001, 0.1)

        def _make_DPLR_HiPPO(N):
            P = np.sqrt(1 + 2 * np.arange(N))
            A = P[:, None] * P[None, :]
            A = np.tril(A) - np.diag(np.arange(N))
            nhippo = -A
            p = 0.5 * np.sqrt(2 * np.arange(1, N + 1) + 1.0)
            q = 2 * p
            S = nhippo + p[:, None] * q[None, :]
            Lambda, V = np.linalg.eig(S)
            Vc = V.conj().T
            p_t = Vc @ p
            q_t = Vc @ q.conj()
            return (Lambda, p_t, q_t, Vc)

        def _ri(z):
            return np.stack([z.real, z.imag], axis=-1).astype(np.float32)

        def _cplx(x_ri):
            return x_ri[..., 0] + 1j * x_ri[..., 1]

        def _s4_kernel(Lambda, p, q, B, Ct, step, L):
            Omega = jnp.exp(-2j * jnp.pi * (jnp.arange(L) / L))
            g = 2.0 / step * ((1.0 - Omega) / (1.0 + Omega))
            c = 2.0 / (1.0 + Omega)
            denom = g[:, None] - Lambda[None, :]
            cauchy = lambda v: (v[None, :] / denom).sum(-1)
            k00 = cauchy(Ct.conj() * B)
            k01 = cauchy(Ct.conj() * p)
            k10 = cauchy(q.conj() * B)
            k11 = cauchy(q.conj() * p)
            at_roots = c * (k00 - k01 * (1.0 / (1.0 + k11)) * k10)
            return jnp.fft.ifft(at_roots, L).real
        L = u.shape[-1]
        Lambda = _cplx(Lambda_ri)
        p = _cplx(p_ri)
        q = _cplx(q_ri)
        Vc = _cplx(Vc_ri)
        Ct = _cplx(Ct_ri).reshape(-1)
        B = (Vc @ Bp.astype(Vc.dtype)).reshape(-1)
        step = jnp.exp(log_step)[0]
        K = _s4_kernel(Lambda, p, q, B, Ct, step, L).astype(u.dtype)
        n = 2 * L
        y = jnp.fft.irfft(jnp.fft.rfft(u, n=n) * jnp.fft.rfft(K, n=n), n=n)[..., :L]
        return y + D[0] * u

    def _L0_ffn_ref(x, route_w, A, Bw):
        import jax, jax.numpy as jnp
        import numpy as np
        R = 16
        LORA_ALPHA = 16
        SCALING = LORA_ALPHA / R
        logits = jnp.einsum('bsd,ed->bse', x, route_w)
        topk_v, topk_idx = jax.lax.top_k(logits, 1)
        E = logits.shape[-1]
        route_weight = jax.nn.one_hot(topk_idx[..., 0], E, dtype=logits.dtype) * topk_v
        h = jnp.einsum('bsd,erd->bser', x, A)
        wh = route_weight[..., None] * h
        out = jnp.einsum('bser,eor->bso', wh, Bw) * SCALING
        return out
    h = _L0_tok_ref(x, L0_tok_orig_emb_w, L0_tok_new_emb)
    h = h + _L0_attn_ref(_layernorm(h, axis=-1), L0_attn_Lambda_ri, L0_attn_p_ri, L0_attn_q_ri, L0_attn_Vc_ri, L0_attn_Ct_ri, L0_attn_Bp, L0_attn_D, L0_attn_log_step)
    h = h + _L0_ffn_ref(_layernorm(h, axis=-1), L0_ffn_route_w, L0_ffn_A, L0_ffn_Bw)
    return h

_drawn_inputs = setup_inputs


def setup_inputs(seed=0):
    import zlib

    import numpy as np

    out = dict(_drawn_inputs(seed))
    spreads = {}
    factors = {'L0_attn_Lambda_ri': 8.0,
     'L0_attn_p_ri': 8.0,
     'L0_attn_q_ri': 8.0,
     'L0_attn_Vc_ri': 8.0,
     'L0_attn_Ct_ri': 8.0,
     'L0_attn_Bp': 8.0}
    for name, (base, spread) in spreads.items():
        noise = np.random.default_rng([zlib.crc32(name.encode()), seed]).standard_normal(out[name].shape)
        drawn = base * np.exp(spread * noise) if base else spread * noise
        out[name] = jnp.asarray(drawn.astype(out[name].dtype))
    for name, factor in factors.items():
        out[name] = (out[name] * factor).astype(out[name].dtype)
    return out
```

```python
from contextlib import ExitStack

import numpy as np

import concourse.bass as bass
from concourse import mybir

P = 128
TOK = 4096
D = 1024
VOCAB = 8192
NB = D // P
NT = TOK // P
E = 8
R = 16
W = E + E * R
NS = 64
EPS = 1e-5
U_SCALE = 1024.0
TOP = 16384.0
H_SCALE = 2.0 ** -20
SLOTS = 4

L_RE, L_IM, P_RE, P_IM, Q_RE, Q_IM, C_RE, C_IM, LOG_STEP, SKIP_D = range(10)

EXP_TERMS = [1.0, 1.0, 1 / 2, 1 / 6, 1 / 24, 1 / 120, 1 / 720, 1 / 5040, 1 / 40320, 1 / 362880]
LN2_HI, LN2_LO = 0.693359375, -2.12194440e-4

(VE1, STD1, R0, T0, T1, SC1, NB1, SG1, NM2, SSQ, VE2, STD2, Q0, Q1, Q2, R2S, R2A, COEF, S2A, S2B, MU1, VAR1) = range(22)
NSC = 24


def build(nc, ids, table, params, vct, bp, w_in, wf_in, bw_in, trig, cos_s, dft, tw, ident_in, expert_in, krows, out):
    f32, f16, i32, u32 = mybir.dt.float32, mybir.dt.float16, mybir.dt.int32, mybir.dt.uint32
    ALU, ACT, AX = mybir.AluOpType, mybir.ActivationFunctionType, mybir.AxisListType.X
    V, S, G, PE = nc.vector, nc.scalar, nc.gpsimd, nc.tensor
    RMAX = bass.bass_isa.ReduceOp.max
    KW = 1280

    ctx = ExitStack()
    with ctx:
        def sb(name, shape, dt=f32):
            return ctx.enter_context(nc.sbuf_tensor(name, shape, dt))

        def pb(name, shape, dt=f32):
            return ctx.enter_context(nc.psum_tensor(name, shape, dt))

        def sem(name):
            return ctx.enter_context(nc.semaphore(name))

        ids_raw = sb("ids_raw", [P, NT], i32)
        ids_ok = sb("ids_ok", [P, NT], i32)
        ids_now = sb("ids_now", [P, SLOTS], i32)
        par = sb("par", [P, 10])
        vct_sb = sb("vct_sb", [NS, 2, P])
        bp_sb = sb("bp_sb", [NS, 1])
        trig_sb = sb("trig_sb", [P, 2, 512])
        cos_sb = sb("cos_sb", [P, NB])
        dft_sb = sb("dft_sb", [P, 2, P])
        tw_sb = sb("tw_sb", [16, D])
        ident = sb("ident", [P, P], f16)
        expert = sb("expert", [P, E * R])
        ones = sb("ones", [P, P])
        mean_w = sb("mean_w", [P, P])
        w_raw = sb("w_raw", [P, NB, W])
        w_fwd = sb("w_fwd", [P, NB, W])
        w_avg = sb("w_avg", [P, W])
        wf_hi = sb("wf_hi", [P, NB, W], f16)
        wf_lo = sb("wf_lo", [P, NB, W], f16)
        bw_raw = sb("bw_raw", [P, D])
        wg_hi = sb("wg_hi", [P, NB, 2 * W], f16)
        wg_lo = sb("wg_lo", [P, NB, 2 * W], f16)
        bw_hi = sb("bw_hi", [P, D], f16)
        bw_lo = sb("bw_lo", [P, D], f16)
        toe_hi = sb("toe_hi", [P, D], f16)
        toe_lo = sb("toe_lo", [P, D], f16)
        g_raw = sb("g_raw", [P, NB, W])
        tiny = sb("tiny", [P, 64])
        tiny_i = sb("tiny_i", [P, 2], i32)
        yv = sb("yv", [P, 4])
        v_all = sb("v_all", [P, 8])
        v_mask = sb("v_mask", [P, 2])
        v_er = sb("v_er", [P, 2, 8])
        v_ei = sb("v_ei", [P, 2, 8])
        d_re = sb("d_re", [P, 512])
        d_im = sb("d_im", [P, 512])
        ti = sb("ti", [P, 512])
        sq_re = sb("sq_re", [P, 512])
        sq_im = sb("sq_im", [P, 512])
        den = sb("den", [P, 512])
        inv = sb("inv", [P, 512])
        e_re = sb("e_re", [P, 512])
        e_im = sb("e_im", [P, 512])
        kap = sb("kap", [P, 8, NB])
        fx = sb("fx", [P, 12, 2, NB])
        f_a = sb("f_a", [P, 2, NB])
        f_b = sb("f_b", [P, 2, NB])
        z_sb = sb("z_sb", [16, P])
        zt = sb("zt", [16, NB, P])
        k_all = sb("k_all", [P, D])
        k_row = sb("k_row", [1, 2, KW], f16)
        cmax = sb("cmax", [P, 4])
        amax = sb("amax", [P, 4])
        scl = sb("scl", [P, 16])
        h0 = sb("h0", [P, SLOTS, D])
        h2 = sb("h2", [P, SLOTS, D])
        u = sb("u", [P, 2, D])
        u_hi = sb("u_hi", [P, 2, D], f16)
        u_lo = sb("u_lo", [P, 2, D], f16)
        ut_hi = sb("ut_hi", [P, 2, D], f16)
        ut_lo = sb("ut_lo", [P, 2, D], f16)
        junk = sb("junk", [P, D])
        bns = sb("bns", [P, SLOTS, 2, 6])
        sc = sb("sc", [P, SLOTS, NSC])
        t_w = sb("t_w", [P, 2, W])
        l_w = sb("l_w", [P, 2, W])
        top8 = sb("top8", [P, 2, 8])
        arg8 = sb("arg8", [P, 2, 8], u32)
        argf = sb("argf", [P, 2, 1])
        sel = sb("sel", [P, 2, E * R])
        sels = sb("sels", [P, 2, E * R])
        wh = sb("wh", [P, 2, 2, P], f16)
        wht = sb("wht", [P, 2, 2, P], f16)

        y = [pb("y0", [P, D]), pb("y1", [P, D])]
        wp = [pb("wp0", [P, 512]), pb("wp1", [P, 512])]
        tr_hi = pb("tr_hi", [P, D], f16)
        tr_lo = pb("tr_lo", [P, D], f16)

        ld = {n: sem("ld_" + n) for n in ("ids", "par", "vct", "bp", "w", "wf", "bw", "trig", "cos", "dft", "tw", "id", "ex")}
        ones_ready, bvec_done, wmean_done = sem("ones_ready"), sem("bvec_done"), sem("wmean_done")
        pre_dve = sem("pre_dve")
        ids_clipped, cos_parts, den_im, squares = sem("ids_clipped"), sem("cos_parts"), sem("den_im"), sem("squares")
        cauchy_in, cauchy_done, spec_ready, z_done = sem("cauchy_in"), sem("cauchy_done"), sem("spec_ready"), sem("z_done")
        zt_ready, k_done, krow_part, krow_stored = sem("zt_ready"), sem("k_done"), sem("krow_part"), sem("krow_stored")
        ld_toe, wavg_ready, w_scale, wf_step = sem("ld_toe"), sem("wavg_ready"), sem("w_scale"), sem("wf_step")
        colmax_ready, max_ready = sem("colmax_ready"), sem("max_ready")
        w_split, g_done, gmax_ready, gtop_ready, weights_ready = (
            sem("w_split"), sem("g_done"), sem("gmax_ready"), sem("gtop_ready"), sem("weights_ready"))
        gathered = [sem(f"gathered{k}") for k in range(SLOTS)]
        stored = [sem(f"stored{k}") for k in range(SLOTS)]
        ids_taken = sem("ids_taken")
        dve_passed, pool_passed = sem("dve_passed"), sem("pool_passed")
        bn_done, aggr_done, var1_ready, std1_ready = sem("bn_done"), sem("aggr_done"), sem("var1_ready"), sem("std1_ready")
        n1a, n1b, n1c, n1d, scale1_ready, u_ready = sem("n1a"), sem("n1b"), sem("n1c"), sem("n1d"), sem("scale1_ready"), sem("u_ready")
        hi_ready, lo_ready = sem("hi_ready"), sem("lo_ready")
        trhi_done, trlo_done, uthi_ready, utlo_ready = sem("trhi_done"), sem("trlo_done"), sem("uthi_ready"), sem("utlo_ready")
        ya_done, main_done = sem("ya_done"), sem("main_done")
        h2_done, negmean2_ready, ssq_ready, std2_ready = sem("h2_done"), sem("negmean2_ready"), sem("ssq_ready"), sem("std2_ready")
        n2s, n2a, n2b, n2c = sem("n2s"), sem("n2a"), sem("n2b"), sem("n2c")
        rt_a, rt_b, rt_c, rt_d, rt_e, rt_f, rt_g = (sem("rt_" + c) for c in "abcdefg")
        whhi_ready, wh_ready, whtr_done, wht_ready = sem("whhi_ready"), sem("wh_ready"), sem("whtr_done"), sem("wht_ready")
        ffn_done, final_done = sem("ffn_done"), sem("final_done")

        block = ctx.enter_context(nc.Block())
        out_t = out.rearrange("(t p) d -> t p d", p=P)

        def slot16(base, off):
            return base * 4 + 16 * (off // SLOTS + 1)

        @block.sync
        def _(sp):
            sp.dma_start(par[:, :], params).then_inc(ld["par"], 16)
            sp.dma_start(trig_sb[:, :, :], trig).then_inc(ld["trig"], 16)
            sp.dma_start(ids_raw[:, :], ids).then_inc(ld["ids"], 16)
            sp.dma_start(w_raw[:, :, :], w_in).then_inc(ld["w"], 16)
            sp.dma_start(w_fwd[:, :, :], wf_in).then_inc(ld["wf"], 16)
            sp.dma_start(dft_sb[:, :, :], dft).then_inc(ld["dft"], 16)
            sp.dma_start(tw_sb[:, :], tw).then_inc(ld["tw"], 16)
            sp.dma_start(ident[:, :], ident_in).then_inc(ld["id"], 16)
            sp.wait_ge(krow_part, 2)
            sp.dma_start(krows[0:1, 0:2 * KW], k_row[0:1, 0:2, :].rearrange("o r x -> o (r x)")).then_inc(krow_stored, 16)
            sp.wait_ge(krow_stored, 16)
            for r, t in enumerate((toe_hi, toe_lo)):
                sp.dma_start(t[:, :], bass.AP(tensor=krows.tensor, offset=r * KW, ap=[[1, P], [1, D]])).then_inc(ld_toe, 16)

            def store(base, off):
                sp.wait_ge(final_done, base + off + 3)
                sp.dma_start(out_t[base + off, :, :], h2[:, off % SLOTS, :]).then_inc(stored[off % SLOTS], 16)

            with sp.Fori(0, NT // SLOTS) as turn:
                first = sp.snap(turn * SLOTS)
                for k in range(SLOTS):
                    store(first, k)
            for k in range(SLOTS):
                sp.wait_ge(stored[k], 16 * (NT // SLOTS + 1))

        @block.gpsimd
        def _(pool):
            for k in range(SLOTS):
                pool.sem_inc(stored[k], 16)
            pool.sem_inc(final_done, 2)
            G.memset(ones[:, :], 1.0)
            G.memset(mean_w[:, :], 1.0 / D)
            G.memset(v_mask[:, :], 0.0)
            G.memset(k_row[:, :, :], 0.0).then_inc(ones_ready, 1)
            pool.wait_ge(ids_clipped, 1)

            def take_ids(base, off):
                k = off % SLOTS
                G.tensor_copy(ids_now[:, k:k + 1], ids_ok[:, bass.ds(base + off, 1)]).then_inc(ids_taken, 1)
                pool.wait_ge(ids_taken, base + off + 1)
                pool.sem_inc(pool_passed, 1)

            def gather(off):
                G.indirect_dma_start(
                    out=h0[:, off % SLOTS, :], out_offset=None, in_=table,
                    in_offset=bass.IndirectOffsetOnAxis(ap=ids_now[:, off % SLOTS:off % SLOTS + 1], axis=0),
                ).then_inc(gathered[off % SLOTS], 16)

            for t in range(SLOTS):
                take_ids(0, t)
                gather(t)
            pool.wait_ge(colmax_ready, 1)
            G.partition_all_reduce(amax[:, 0:2], cmax[:, 0:2], P, RMAX).then_inc(max_ready, 1)
            pool.wait_ge(ld["wf"], 16)
            pool.wait_ge(wavg_ready, 1)
            G.tensor_tensor(w_fwd[:, :, :], w_fwd[:, :, :],
                            w_avg[:, :].rearrange("p (o w) -> p o w", o=1).broadcast_to([P, NB, W]), ALU.subtract).then_inc(wf_step, 1)
            pool.wait_ge(wf_step, 1)
            pool.wait_ge(w_scale, 1)
            G.tensor_scalar(w_fwd[:, :, :], w_fwd[:, :, :], scl[:, 5:6], None, ALU.mult).then_inc(wf_step, 1)
            pool.wait_ge(wf_step, 2)
            G.tensor_copy(wf_hi[:, :, :], w_fwd[:, :, :]).then_inc(wf_step, 1)
            pool.wait_ge(wf_step, 3)
            G.tensor_tensor(wf_lo[:, :, :], w_fwd[:, :, :], wf_hi[:, :, :], ALU.subtract).then_inc(w_split, 1)
            pool.wait_ge(gmax_ready, 1)
            G.partition_all_reduce(amax[:, 2:3], cmax[:, 2:3], P, RMAX).then_inc(gtop_ready, 1)
            with pool.Fori(0, NT // SLOTS - 1) as turn:
                first = pool.snap(turn * SLOTS)
                for k in range(SLOTS):
                    pool.wait_ge(h2_done, first + (k + 1))
                    take_ids(first, k + SLOTS)
                    gather(k + SLOTS)

        @block.scalar
        def _(act):
            act.dma_start(vct_sb[:, :, :], vct).then_inc(ld["vct"], 16)
            act.dma_start(bp_sb[:, :], bp).then_inc(ld["bp"], 16)
            act.dma_start(cos_sb[:, :], cos_s).then_inc(ld["cos"], 16)
            act.dma_start(expert[:, :], expert_in).then_inc(ld["ex"], 16)
            act.dma_start(bw_raw[:, :], bw_in).then_inc(ld["bw"], 16)
            act.wait_ge(ld["par"], 16)
            act.wait_ge(ld["trig"], 16)
            S.activation(ti[:, :], trig_sb[:, 0, :], ACT.Copy, scale=par[:, L_IM:L_IM + 1]).then_inc(cos_parts, 1)
            S.activation(d_re[:, :], trig_sb[:, 0, :], ACT.Copy, scale=par[:, L_RE:L_RE + 1]).then_inc(cos_parts, 1)
            act.wait_ge(cos_parts, 2)
            S.activation(sq_re[:, :], d_re[:, :], ACT.Square).then_inc(squares, 1)
            act.wait_ge(den_im, 1)
            S.activation(sq_im[:, :], d_im[:, :], ACT.Square).then_inc(squares, 1)
            def root1(base, off):
                k = off % SLOTS
                act.wait_ge(var1_ready, base + off + 1)
                S.activation(sc[:, k, STD1:STD1 + 1], sc[:, k, VE1:VE1 + 1], ACT.Sqrt).then_inc(std1_ready, 1)

            def split_hi(base, off):
                k = off % SLOTS
                act.wait_ge(scale1_ready, base + off + 1)
                S.activation(u_hi[:, off % 2, :], h0[:, k, ::-1], ACT.Identity, bias=sc[:, k, NB1:NB1 + 1],
                             scale=sc[:, k, SC1:SC1 + 1]).then_inc(hi_ready, 1)

            def copy_transposed(base, off):
                act.wait_ge(trhi_done, base + off + 1)
                S.copy(ut_hi[:, off % 2, :], tr_hi[:, :]).then_inc(uthi_ready, 1)
                act.wait_ge(trlo_done, base + off + 1)
                S.copy(ut_lo[:, off % 2, :], tr_lo[:, :]).then_inc(utlo_ready, 1)

            def squares2(base, off):
                k = off % SLOTS
                act.wait_ge(negmean2_ready, base + off + 1)
                S.activation(junk[:, :], h2[:, k, :], ACT.Square, bias=sc[:, k, NM2:NM2 + 1],
                             accum_out=sc[:, k, SSQ:SSQ + 1]).then_inc(ssq_ready, 1)

            def root2(base, off):
                k = off % SLOTS
                act.wait_ge(n2s, base + off + 1)
                S.activation(sc[:, k, STD2:STD2 + 1], sc[:, k, VE2:VE2 + 1], ACT.Sqrt).then_inc(std2_ready, 1)

            def copy_wh(base, off):
                act.wait_ge(whtr_done, base + off + 1)
                S.copy(wht[:, off % 2, :, :], wp[off % 2][:, 288:416].bitcast(f16)).then_inc(wht_ready, 1)

            def step(base, off, before=True, stage=True, turn=True):
                if before:
                    squares2(base, off - 1)
                    root2(base, off - 1)
                if stage:
                    root1(base, off + 2)
                if turn:
                    if off or base is not 0:
                        act.wait_ge(main_done, base + off)
                    copy_transposed(base, off + 1)
                if stage:
                    split_hi(base, off + 2)
                if before:
                    copy_wh(base, off - 1)

            root1(0, 0)
            split_hi(0, 0)
            root1(0, 1)
            split_hi(0, 1)
            copy_transposed(0, 0)
            step(0, 0, before=False)
            with act.Fori(0, NT // SLOTS - 1) as turn:
                first = act.snap(turn * SLOTS)
                for k in range(SLOTS):
                    step(first, k + 1)
            step(0, NT - 3)
            step(0, NT - 2, stage=False)
            step(0, NT - 1, stage=False, turn=False)
            step(0, NT, stage=False, turn=False)

        @block.vector
        def _(dve):
            steps = [0]

            def link(ins):
                steps[0] += 1
                ins.then_inc(pre_dve, 1)
                dve.wait_ge(pre_dve, steps[0])

            def c(j, n=1):
                return tiny[:, j:j + n]

            dve.wait_ge(ld["ids"], 16)
            V.tensor_scalar(ids_ok[:, :], ids_raw[:, :], 0, VOCAB - 1, ALU.max, ALU.min).then_inc(ids_clipped, 1)
            dve.wait_ge(ld["par"], 16)
            link(V.tensor_scalar(c(0), par[:, LOG_STEP:LOG_STEP + 1], -1.0, 87.0, ALU.mult, ALU.min))
            link(V.tensor_scalar(c(0), c(0), -87.0, None, ALU.max))
            link(V.tensor_scalar(tiny_i[:, 0:1], c(0), 1.4426950408889634, None, ALU.mult))
            link(V.tensor_copy(c(1), tiny_i[:, 0:1]))
            link(V.scalar_tensor_tensor(c(2), c(1), -LN2_HI, c(0), ALU.mult, ALU.add))
            link(V.scalar_tensor_tensor(c(2), c(1), -LN2_LO, c(2), ALU.mult, ALU.add))
            V.memset(c(3), EXP_TERMS[-1])
            link(V.tensor_scalar(tiny_i[:, 0:1], c(1), 128.0, None, ALU.add))
            link(V.tensor_scalar(tiny_i[:, 1:2], tiny_i[:, 0:1], 23, None, ALU.logical_shift_left))
            for term in EXP_TERMS[-2::-1]:
                link(V.tensor_scalar(c(3), c(3), c(2), term, ALU.mult, ALU.add))
            link(V.tensor_tensor(c(4), c(3), tiny_i[:, 1:2].bitcast(f32), ALU.mult))
            dve.wait_ge(cos_parts, 1)
            V.scalar_tensor_tensor(d_im[:, :], trig_sb[:, 1, :], c(4), ti[:, :], ALU.mult, ALU.subtract).then_inc(den_im, 1)
            dve.wait_ge(ones_ready, 1)
            V.memset(v_mask[0:64, 0:1], 1.0)
            V.memset(v_mask[64:128, 1:2], 1.0)
            V.tensor_copy(yv[:, 1:4:2], par[:, P_RE:P_IM + 1])
            dve.wait_ge(bvec_done, 1)
            link(V.tensor_copy(yv[:, 0:3:2], wp[1][:, 0:2]))
            for i, (re, im) in enumerate(((C_RE, C_IM), (Q_RE, Q_IM))):
                xr, xi = par[:, re:re + 1], par[:, im:im + 1]
                V.tensor_scalar(c(8 + 4 * i, 2), yv[:, 2:4], xi, None, ALU.mult)
                link(V.tensor_scalar(c(10 + 4 * i, 2), yv[:, 0:2], xi, None, ALU.mult))
                V.scalar_tensor_tensor(v_all[:, 2 * i:2 * i + 2], yv[:, 0:2], xr, c(8 + 4 * i, 2), ALU.mult, ALU.add)
                link(V.scalar_tensor_tensor(v_all[:, 4 + 2 * i:6 + 2 * i], yv[:, 2:4], xr, c(10 + 4 * i, 2), ALU.mult, ALU.subtract))
            for h in range(2):
                m = v_mask[:, h:h + 1]
                V.tensor_scalar(v_er[:, h, :], v_all[:, :], m, None, ALU.mult)
                V.tensor_scalar(v_ei[:, h, 0:4], v_all[:, 4:8], m, None, ALU.mult)
                last = V.tensor_scalar(v_ei[:, h, 4:8], v_all[:, 0:4], m, -1.0, ALU.mult, ALU.mult)
            link(last)
            dve.wait_ge(squares, 2)
            link(V.tensor_tensor(den[:, :], sq_re[:, :], sq_im[:, :], ALU.add))
            link(V.reciprocal(inv[:, :], den[:, :]))
            V.scalar_tensor_tensor(e_re[:, :], d_re[:, :], -1.0, inv[:, :], ALU.mult, ALU.mult)
            V.tensor_tensor(e_im[:, :], d_im[:, :], inv[:, :], ALU.mult).then_inc(cauchy_in, 1)
            dve.wait_ge(wmean_done, 1)
            dve.wait_ge(ld["w"], 16)
            V.tensor_copy(w_avg[:, :], wp[0][:, 0:W]).then_inc(wavg_ready, 1)
            dve.wait_ge(wavg_ready, 1)
            link(V.tensor_tensor(w_raw[:, :, :], w_raw[:, :, :],
                                 w_avg[:, :].rearrange("p (o w) -> p o w", o=1).broadcast_to([P, NB, W]), ALU.subtract))
            V.tensor_reduce(cmax[:, 0:1], w_raw[:, :, :].rearrange("p b w -> p (b w)"), AX, ALU.max, apply_absolute_value=True)
            dve.wait_ge(ld["bw"], 16)
            V.tensor_reduce(cmax[:, 1:2], bw_raw[:, :], AX, ALU.max, apply_absolute_value=True).then_inc(colmax_ready, 1)
            dve.wait_ge(cauchy_done, 1)
            link(V.tensor_copy(kap[:, :, :], y[0][:, 0:64].rearrange("p (f c) -> p c f", c=8)))
            dve.wait_ge(ld["cos"], 16)

            def pair(j):
                return kap[:, j:j + 5:4, :]

            def both(x):
                return x.rearrange("p (o f) -> p o f", o=1).broadcast_to([P, 2, NB])

            cosb = both(cos_sb[:, :])
            V.tensor_tensor(fx[:, 0, :, :], pair(1), both(kap[:, 2, :]), ALU.mult)
            V.tensor_tensor(fx[:, 1, :, :], pair(1), both(kap[:, 6, :]), ALU.mult)
            link(V.tensor_tensor(fx[:, 2, :, :], pair(3), cosb, ALU.mult))
            V.tensor_tensor(fx[:, 3, 0, :], fx[:, 0, 0, :], fx[:, 1, 1, :], ALU.subtract)
            V.tensor_tensor(fx[:, 3, 1, :], fx[:, 0, 1, :], fx[:, 1, 0, :], ALU.add)
            link(V.tensor_scalar(fx[:, 2, 0, :], fx[:, 2, 0, :], 1.0, None, ALU.add))
            V.tensor_tensor(fx[:, 5, :, :], fx[:, 2, :, :], fx[:, 2, :, :], ALU.mult)
            link(V.tensor_tensor(fx[:, 4, :, :], fx[:, 3, :, :], cosb, ALU.mult))
            V.tensor_tensor(fx[:, 6, 0, :], fx[:, 5, 0, :], fx[:, 5, 1, :], ALU.add)
            V.tensor_tensor(fx[:, 7, :, :], fx[:, 4, :, :], both(fx[:, 2, 0, :]), ALU.mult)
            link(V.tensor_tensor(fx[:, 8, :, :], fx[:, 4, :, :], both(fx[:, 2, 1, :]), ALU.mult))
            V.reciprocal(fx[:, 6, 1, :], fx[:, 6, 0, :])
            V.tensor_tensor(fx[:, 9, 0, :], fx[:, 7, 0, :], fx[:, 8, 1, :], ALU.add)
            link(V.tensor_tensor(fx[:, 9, 1, :], fx[:, 7, 1, :], fx[:, 8, 0, :], ALU.subtract))
            link(V.tensor_tensor(fx[:, 10, :, :], fx[:, 9, :, :], both(fx[:, 6, 1, :]), ALU.mult))
            link(V.tensor_tensor(f_a[:, :, :], pair(0), fx[:, 10, :, :], ALU.subtract))
            V.tensor_scalar(f_b[:, 0, :], f_a[:, 1, :], -1.0, None, ALU.mult)
            V.tensor_copy(f_b[:, 1, :], f_a[:, 0, :]).then_inc(spec_ready, 1)
            dve.wait_ge(z_done, 1)
            dve.wait_ge(ld["tw"], 16)
            V.tensor_tensor(zt[:, :, :], tw_sb[:, :].rearrange("q (a b) -> q a b", b=P),
                            y[0][0:16, 512:640].rearrange("q (o b) -> q o b", o=1).broadcast_to([16, NB, P]),
                            ALU.mult).then_inc(zt_ready, 1)
            dve.wait_ge(k_done, 1)
            link(V.tensor_copy(k_all[:, :], y[1][:, :]))
            link(V.tensor_tensor(k_all[:, 0:1], k_all[:, 0:1], par[:, SKIP_D:SKIP_D + 1], ALU.add))
            link(V.tensor_reduce(scl[:, 0:1], k_all[:, :], AX, ALU.max, apply_absolute_value=True))
            link(V.tensor_scalar(scl[:, 1:2], scl[:, 0:1], 1e-30, 1.0 / TOP, ALU.max, ALU.mult))
            link(V.reciprocal(scl[:, 2:3], scl[:, 1:2]))
            link(V.tensor_scalar(k_all[0:1, :], k_all[0:1, :], scl[0:1, 2:3], None, ALU.mult))
            V.tensor_copy(k_row[0:1, 0, P - 1:P - 1 + D], k_all[0:1, :]).then_inc(krow_part, 1)
            dve.wait_ge(krow_part, 1)
            V.tensor_tensor(k_row[0:1, 1, P - 1:P - 1 + D], k_all[0:1, :], k_row[0:1, 0, P - 1:P - 1 + D], ALU.subtract).then_inc(krow_part, 1)
            dve.wait_ge(max_ready, 1)
            link(V.tensor_scalar(scl[:, 3:5], amax[:, 0:2], 1e-30, 1.0 / TOP, ALU.max, ALU.mult))
            V.reciprocal(scl[:, 5:7], scl[:, 3:5]).then_inc(w_scale, 1)
            dve.wait_ge(w_scale, 1)
            link(V.tensor_scalar(w_raw[:, :, :], w_raw[:, :, :], scl[:, 5:6], None, ALU.mult))
            link(V.tensor_copy(wg_hi[:, :, 0:W], w_raw[:, :, :]))
            link(V.tensor_tensor(wg_lo[:, :, 0:W], w_raw[:, :, :], wg_hi[:, :, 0:W], ALU.subtract))
            link(V.tensor_scalar(bw_raw[:, :], bw_raw[:, :], scl[:, 6:7], None, ALU.mult))
            link(V.tensor_copy(bw_hi[:, :], bw_raw[:, :]))
            link(V.tensor_tensor(bw_lo[:, :], bw_raw[:, :], bw_hi[:, :], ALU.subtract))
            V.tensor_scalar(scl[:, 7:8], scl[:, 1:2], 1.0 / U_SCALE, None, ALU.mult)
            link(V.tensor_tensor(scl[:, 8:9], scl[:, 3:4], scl[:, 4:5], ALU.mult))

            def stats1(base, off):
                k, n = off % SLOTS, base + off + 1
                dve.wait_ge(gathered[k], slot16(base, off))
                V.bn_stats(bns[:, k, 0, :], h0[:, k, 0:512])
                V.bn_stats(bns[:, k, 1, :], h0[:, k, 512:1024]).then_inc(bn_done, 1)
                dve.wait_ge(bn_done, n)
                dve.sem_inc(dve_passed, 1)
                V.bn_aggr(sc[:, k, MU1:MU1 + 2], bns[:, k, :, :]).then_inc(aggr_done, 1)
                dve.wait_ge(aggr_done, n)
                V.tensor_scalar(sc[:, k, VE1:VE1 + 1], sc[:, k, VAR1:VAR1 + 1], EPS, None, ALU.add).then_inc(var1_ready, 1)

            def norm1(base, off):
                k, n = off % SLOTS, base + off + 1

                def s(j):
                    return sc[:, k, j:j + 1]

                dve.wait_ge(std1_ready, n)
                V.reciprocal(s(R0), s(STD1)).then_inc(n1a, 1)
                dve.wait_ge(n1a, n)
                V.tensor_scalar(s(T0), s(VE1), s(R0), s(R0), ALU.mult, ALU.mult).then_inc(n1b, 1)
                dve.wait_ge(n1b, n)
                V.tensor_scalar(s(T1), s(T0), -0.5, 1.5, ALU.mult, ALU.add).then_inc(n1c, 1)
                dve.wait_ge(n1c, n)
                V.tensor_scalar(s(SC1), s(T1), s(R0), U_SCALE, ALU.mult, ALU.mult).then_inc(n1d, 1)
                dve.wait_ge(n1d, n)
                V.tensor_scalar(s(NB1), s(MU1), s(SC1), -1.0, ALU.mult, ALU.mult)
                V.tensor_scalar(s(SG1), s(VE1), s(SC1), 1.0 / U_SCALE, ALU.mult, ALU.mult).then_inc(scale1_ready, 1)
                V.tensor_scalar(u[:, off % 2, :], h0[:, k, ::-1], s(MU1), s(SC1), ALU.subtract, ALU.mult).then_inc(u_ready, 1)

            def split_lo(base, off):
                n = base + off + 1
                dve.wait_ge(u_ready, n)
                dve.wait_ge(hi_ready, n)
                V.tensor_tensor(u_lo[:, off % 2, :], u[:, off % 2, :], u_hi[:, off % 2, :], ALU.subtract).then_inc(lo_ready, 1)

            def residual(base, off, half):
                k, a = off % SLOTS, 512 * half
                if half:
                    dve.wait_ge(main_done, base + off + 1)
                else:
                    dve.wait_ge(ya_done, base + off + 1)
                    dve.wait_ge(stored[k], slot16(base, off))
                last = V.scalar_tensor_tensor(h2[:, k, a:a + 512], y[off % 2][:, a:a + 512], scl[:, 7:8],
                                              h0[:, k, a:a + 512], ALU.mult, ALU.add,
                                              accum_out=sc[:, k, S2A + half:S2A + half + 1])
                if half:
                    last.then_inc(h2_done, 1)

            def route(base, off):
                k, b, n = off % SLOTS, off % 2, base + off + 1
                dve.wait_ge(h2_done, n)
                V.tensor_scalar(sc[:, k, NM2:NM2 + 1], sc[:, k, S2A:S2A + 1], sc[:, k, S2B:S2B + 1], -1.0 / D,
                                ALU.add, ALU.mult).then_inc(negmean2_ready, 1)
                V.tensor_scalar(t_w[:, b, :], wp[b][:, 0:W], sc[:, k, SG1:SG1 + 1], None, ALU.mult).then_inc(rt_a, 1)
                dve.wait_ge(rt_a, n)
                V.scalar_tensor_tensor(l_w[:, b, :], wp[b][:, W:2 * W], scl[:, 9:10], t_w[:, b, :],
                                       ALU.mult, ALU.add).then_inc(rt_b, 1)
                dve.wait_ge(rt_b, n)
                dve.sem_inc(dve_passed, 1)
                V.max(top8[:, b, :], l_w[:, b, 0:E]).then_inc(rt_c, 1)
                dve.wait_ge(rt_c, n)
                dve.sem_inc(dve_passed, 1)
                V.max_index(arg8[:, b, :], top8[:, b, :], l_w[:, b, 0:E]).then_inc(rt_d, 1)
                dve.wait_ge(rt_d, n)
                V.tensor_copy(argf[:, b, :], arg8[:, b, 0:1]).then_inc(rt_e, 1)
                dve.wait_ge(rt_e, n)
                V.scalar_tensor_tensor(sel[:, b, :], expert[:, :], argf[:, b, :], l_w[:, b, E:W],
                                       ALU.is_equal, ALU.mult).then_inc(rt_f, 1)

            def variance2(base, off):
                k, n = off % SLOTS, base + off + 1
                dve.wait_ge(ssq_ready, n)
                V.tensor_scalar(sc[:, k, VE2:VE2 + 1], sc[:, k, SSQ:SSQ + 1], 1.0 / D, EPS, ALU.mult, ALU.add).then_inc(n2s, 1)

            def norm2(base, off):
                k, b, n = off % SLOTS, off % 2, base + off + 1

                def s(j):
                    return sc[:, k, j:j + 1]

                dve.wait_ge(std2_ready, n)
                V.reciprocal(s(Q0), s(STD2)).then_inc(n2a, 1)
                dve.wait_ge(n2a, n)
                V.tensor_scalar(s(Q1), s(VE2), s(Q0), s(Q0), ALU.mult, ALU.mult).then_inc(n2b, 1)
                dve.wait_ge(n2b, n)
                V.tensor_scalar(s(Q2), s(Q1), -0.5, 1.5, ALU.mult, ALU.add).then_inc(n2c, 1)
                dve.wait_ge(n2c, n)
                V.tensor_scalar(s(R2A), s(Q2), s(Q0), scl[:, 3:4], ALU.mult, ALU.mult)
                V.tensor_scalar(s(R2S), s(Q2), s(Q0), H_SCALE, ALU.mult, ALU.mult).then_inc(rt_g, 1)
                dve.wait_ge(rt_f, n)
                dve.wait_ge(rt_g, n)
                V.tensor_scalar(sels[:, b, :], sel[:, b, :], s(R2S), None, ALU.mult).then_inc(whhi_ready, 1)
                dve.wait_ge(whhi_ready, 2 * n - 1)
                V.tensor_copy(wh[:, b, 0, :], sels[:, b, :]).then_inc(whhi_ready, 1)
                V.tensor_scalar(s(COEF), top8[:, b, 0:1], s(R2A), scl[:, 8:9], ALU.mult, ALU.mult)
                dve.wait_ge(whhi_ready, 2 * n)
                V.tensor_tensor(wh[:, b, 1, :], sels[:, b, :], wh[:, b, 0, :], ALU.subtract).then_inc(wh_ready, 1)

            def final(base, off):
                k, n = off % SLOTS, base + off + 1
                dve.wait_ge(ffn_done, n)
                dve.wait_ge(ssq_ready, n)
                for a in (0, 512):
                    last = V.scalar_tensor_tensor(h2[:, k, a:a + 512], y[off % 2][:, a:a + 512], sc[:, k, COEF:COEF + 1],
                                                  h2[:, k, a:a + 512], ALU.mult, ALU.add)
                last.then_inc(final_done, 1)

            for t in range(2):
                stats1(0, t)
                norm1(0, t)
                split_lo(0, t)
            dve.wait_ge(g_done, 1)
            link(V.tensor_copy(g_raw[:, 0:3, :], y[0][:, 0:3 * W].rearrange("p (b w) -> p b w", w=W)))
            link(V.tensor_copy(g_raw[:, 3:6, :], y[0][:, 512:512 + 3 * W].rearrange("p (b w) -> p b w", w=W)))
            link(V.tensor_copy(g_raw[:, 6:8, :], y[1][:, 0:2 * W].rearrange("p (b w) -> p b w", w=W)))
            V.tensor_reduce(cmax[:, 2:3], g_raw[:, :, :].rearrange("p b w -> p (b w)"), AX, ALU.max,
                            apply_absolute_value=True).then_inc(gmax_ready, 1)
            dve.wait_ge(gtop_ready, 1)
            link(V.tensor_scalar(scl[:, 10:11], amax[:, 2:3], 1e-30, 1.0 / TOP, ALU.max, ALU.mult))
            V.tensor_tensor(scl[:, 9:10], scl[:, 10:11], scl[:, 1:2], ALU.mult)
            link(V.reciprocal(scl[:, 11:12], scl[:, 10:11]))
            link(V.tensor_scalar(g_raw[:, :, :], g_raw[:, :, :], scl[:, 11:12], None, ALU.mult))
            link(V.tensor_copy(wg_hi[:, :, W:2 * W], g_raw[:, :, :]))
            V.tensor_tensor(wg_lo[:, :, W:2 * W], g_raw[:, :, :], wg_hi[:, :, W:2 * W], ALU.subtract).then_inc(weights_ready, 1)

            def step(base, off, before=True, stage=True, own=True):
                if before:
                    residual(base, off - 1, 1)
                    route(base, off - 1)
                if stage:
                    stats1(base, off + 2)
                if before:
                    variance2(base, off - 1)
                    norm2(base, off - 1)
                if stage:
                    norm1(base, off + 2)
                    split_lo(base, off + 2)
                if own:
                    residual(base, off, 0)
                if before:
                    final(base, off - 1)

            dve.wait_ge(ld["ex"], 16)
            step(0, 0, before=False)
            with dve.Fori(0, NT // SLOTS - 1) as turn:
                first = dve.snap(turn * SLOTS)
                for k in range(SLOTS):
                    step(first, k + 1)
            step(0, NT - 3)
            step(0, NT - 2, stage=False)
            step(0, NT - 1, stage=False)
            step(0, NT, stage=False, own=False)

        @block.tensor
        def _(pe):
            pe.wait_ge(ld["vct"], 16)
            pe.wait_ge(ld["bp"], 16)
            for c in range(2):
                last = PE.matmul(wp[1][:, c:c + 1], vct_sb[:, c, :], bp_sb[:, :], start=True, stop=True)
            last.then_inc(bvec_done, 1)
            pe.wait_ge(ld["w"], 16)
            pe.wait_ge(ones_ready, 1)
            for b in range(NB):
                last = PE.matmul(wp[0][:, 0:W], mean_w[:, :], w_raw[:, b, :], start=(b == 0), stop=(b == NB - 1))
            last.then_inc(wmean_done, 1)
            pe.wait_ge(cauchy_in, 1)
            for g in range(4):
                o = y[0][:, 16 * g:16 * g + 16]
                PE.matmul(o, e_re[:, P * g:P * g + P], v_er[:, :, :].rearrange("p h c -> p (h c)"), start=True, stop=False)
                last = PE.matmul(o, e_im[:, P * g:P * g + P], v_ei[:, :, :].rearrange("p h c -> p (h c)"), start=False, stop=True)
            last.then_inc(cauchy_done, 1)
            pe.wait_ge(spec_ready, 1)
            pe.wait_ge(ld["dft"], 16)
            PE.matmul(y[0][0:16, 512:640], f_a[:, :, :].rearrange("p a f -> p (a f)"), dft_sb[:, 0, :], start=True, stop=False)
            PE.matmul(y[0][0:16, 512:640], f_b[:, :, :].rearrange("p a f -> p (a f)"), dft_sb[:, 1, :],
                      start=False, stop=True).then_inc(z_done, 1)
            pe.wait_ge(zt_ready, 1)
            ztf = zt[:, :, :].rearrange("q a b -> q (a b)")
            for a in (0, 512):
                last = PE.matmul(y[1][:, a:a + 512], ones[0:16, :], ztf[:, a:a + 512], start=True, stop=True)
            last.then_inc(k_done, 1)

            def transpose_part(base, off, part, bank, ready, free, done):
                pe.wait_ge(ready, base + off + 1)
                if off or base is not 0:
                    pe.wait_ge(free, base + off)
                for b in range(NB):
                    last = PE.transpose(bank[:, b * P:(b + 1) * P], part[:, off % 2, b * P:(b + 1) * P], ident[:, :])
                last.then_inc(done, 1)

            def transpose_u(base, off):
                transpose_part(base, off, u_hi, tr_hi, hi_ready, uthi_ready, trhi_done)
                transpose_part(base, off, u_lo, tr_lo, lo_ready, utlo_ready, trlo_done)

            def conv_block(off, jb, part, weights, wcols):
                yb, first = y[off % 2], jb == 0 and part is ut_hi and weights is toe_hi
                x = part[:, off % 2, D - (jb + 1) * P:D - jb * P]
                last = None
                if jb < 4:
                    last = PE.matmul(yb[:, jb * P:512], x, weights[:, 0:512 - jb * P], start=first, stop=False,
                                     skip_group_check=True)
                a = max(512, jb * P)
                PE.matmul(yb[:, a:D], x, weights[:, a - jb * P:D - jb * P], start=first, stop=False, skip_group_check=True)
                w = PE.matmul(wp[off % 2][:, 0:2 * W], x, wcols[:, jb, :], start=first,
                              stop=False, skip_group_check=True)
                return last, w

            def conv(off, jb):
                conv_block(off, jb, ut_hi, toe_hi, wg_hi)
                conv_block(off, jb, ut_hi, toe_lo, wg_lo)
                return conv_block(off, jb, ut_lo, toe_hi, wg_hi)

            def transpose_wh(base, off):
                b = off % 2
                pe.wait_ge(wh_ready, base + off + 1)
                o = wp[b][:, 288:416].bitcast(f16)
                PE.transpose(o[:, 0:P], wh[:, b, 0, :], ident[:, :])
                PE.transpose(o[:, P:2 * P], wh[:, b, 1, :], ident[:, :]).then_inc(whtr_done, 1)

            def experts(base, off):
                b = off % 2
                pe.wait_ge(wht_ready, base + off + 1)
                for a in (0, 512):
                    o = y[b][:, a:a + 512]
                    PE.matmul(o, wht[:, b, 0, :], bw_hi[:, a:a + 512], start=True, stop=False)
                    PE.matmul(o, wht[:, b, 0, :], bw_lo[:, a:a + 512], start=False, stop=False)
                    last = PE.matmul(o, wht[:, b, 1, :], bw_hi[:, a:a + 512], start=False, stop=True)
                last.then_inc(ffn_done, 1)

            def step(base, off, before=True, turn=True, own=True):
                if own:
                    pe.wait_ge(uthi_ready, base + off + 1)
                    pe.wait_ge(utlo_ready, base + off + 1)
                    pe.wait_ge(final_done, base + off + 1)
                    conv(off, 0)
                    conv(off, 1)
                if turn:
                    transpose_u(base, off + 1)
                if own:
                    conv(off, 2)
                    ya = conv(off, 3)[1]
                    ya.then_inc(ya_done, 1)
                if before:
                    transpose_wh(base, off - 1)
                if own:
                    conv(off, 4)
                if before:
                    experts(base, off - 1)
                if own:
                    conv(off, 5)
                    conv(off, 6)
                    conv(off, 7)[1].then_inc(main_done, 1)

            pe.wait_ge(ld["id"], 16)
            transpose_u(0, 0)
            pe.wait_ge(ld_toe, 32)
            pe.wait_ge(w_split, 1)
            for jb in range(NB):
                bank, at = (y[0], jb * W) if jb < 3 else (y[0], 512 + (jb - 3) * W) if jb < 6 else (y[1], (jb - 6) * W)
                o = bank[:, at:at + W]
                todo = [(tt, ww, lb) for lb in range(jb, NB)
                        for tt, ww in ((toe_hi, wf_hi), (toe_hi, wf_lo), (toe_lo, wf_hi))]
                for i, (tt, ww, lb) in enumerate(todo):
                    d = (lb - jb) * P
                    last = PE.matmul(o, tt[:, d:d + P], ww[:, lb, :], start=(i == 0), stop=(i == len(todo) - 1))
            last.then_inc(g_done, 1)
            pe.wait_ge(weights_ready, 1)
            step(0, 0, before=False)
            with pe.Fori(0, NT // SLOTS - 1) as turn:
                first = pe.snap(turn * SLOTS)
                for k in range(SLOTS):
                    step(first, k + 1)
            step(0, NT - 3)
            step(0, NT - 2)
            step(0, NT - 1, turn=False)
            step(0, NT, turn=False, own=False)


def constants():
    lp = np.arange(P, dtype=np.float64)
    res = np.array([4 * h + g for g in range(4) for h in range(2)], dtype=np.float64)
    half = np.arange(P) // NS
    bins = 8 * lp[None, None, :] + 4 * half[:, None, None] + np.arange(4)[None, :, None]
    phi = np.pi * bins / D
    cosphi = np.where(bins == D // 2, 0.0, np.cos(phi))
    trig = np.stack([cosphi.reshape(P, 512), np.sin(phi).reshape(P, 512)], 1)
    b2 = 8 * lp[:, None] + res[None, :]
    cos_s = np.where(b2 == D // 2, 0.0, np.cos(np.pi * b2 / D))
    t1 = np.arange(P)
    ang = np.pi * ((lp[:, None].astype(np.int64) * (2 * t1[None, :] + 1)) % 256) / 128
    dft = np.stack([np.cos(ang), np.sin(ang)], 1)
    t = np.arange(D)
    th = np.pi * ((res[:, None].astype(np.int64) * (2 * t[None, :] + 1)) % (2 * D)) / D
    tw = np.concatenate([np.cos(th), -np.sin(th)], 0) / D
    expert = np.broadcast_to(np.arange(E * R) // R, (P, E * R))
    f = np.float32
    return trig.astype(f), cos_s.astype(f), dft.astype(f), tw.astype(f), np.eye(P, dtype=np.float16), expert.astype(f)


def kernel(x, L0_tok_orig_emb_w, L0_tok_new_emb, L0_attn_Lambda_ri, L0_attn_p_ri, L0_attn_q_ri, L0_attn_Vc_ri,
           L0_attn_Ct_ri, L0_attn_Bp, L0_attn_D, L0_attn_log_step, L0_ffn_route_w, L0_ffn_A, L0_ffn_Bw):
    import concourse.bacc as bacc
    from concourse.bass_utils import run_bass_kernel_spmd

    def a(v):
        return np.asarray(v)

    trig, cos_s, dft, tw, ident, expert = constants()
    lam, p, q, ct = (a(v).reshape(NS, 2) for v in (L0_attn_Lambda_ri, L0_attn_p_ri, L0_attn_q_ri, L0_attn_Ct_ri))
    cols = np.concatenate([lam, p, q, ct], 1)
    ends = np.broadcast_to(np.stack([a(L0_attn_log_step)[0], a(L0_attn_D)[0]]), (P, 2))
    params = np.concatenate([np.concatenate([cols, cols], 0), ends], 1)
    vct = a(L0_attn_Vc_ri).transpose(1, 2, 0)
    w = np.concatenate([a(L0_ffn_route_w).T, a(L0_ffn_A).reshape(E * R, D).T], 1)
    arrays = {
        "ids": a(x).reshape(NT, P).T,
        "table": np.concatenate([a(L0_tok_orig_emb_w), a(L0_tok_new_emb)], 0),
        "params": params,
        "vct": np.concatenate([vct, vct], 2),
        "bp": a(L0_attn_Bp),
        "w": w.reshape(NB, P, W)[:, ::-1].transpose(1, 0, 2),
        "wf": w.reshape(NB, P, W).transpose(1, 0, 2),
        "bw": a(L0_ffn_Bw).transpose(0, 2, 1).reshape(E * R, D),
        "trig": trig, "cos_s": cos_s, "dft": dft, "tw": tw, "ident": ident, "expert": expert,
    }
    arrays = {f"in_{n}": np.ascontiguousarray(v) for n, v in arrays.items()}
    nc = bacc.Bacc("TRN2", target_bir_lowering=False, num_devices=1)
    args = [nc.dram_tensor(n, v.shape, mybir.dt.from_np(v.dtype), kind="ExternalInput").ap() for n, v in arrays.items()]
    krows = nc.dram_tensor("krows", (1, 2 * 1280), mybir.dt.float16, kind="Internal").ap()
    out = nc.dram_tensor("out_rows", (TOK, D), mybir.dt.float32, kind="ExternalOutput").ap()
    build(nc, *args, krows, out)
    r = run_bass_kernel_spmd(nc, [arrays], core_ids=[0])
    return r.results[0]["out_rows"].reshape(8, 512, D)
```

```python
from contextlib import ExitStack

import numpy as np

import concourse.bass as bass
from concourse import mybir

P = 128
TOK = 4096
D = 1024
VOCAB = 8192
NB = D // P
NT = TOK // P
E = 8
R = 16
W = E + E * R
NS = 64
EPS = 1e-5
U_SCALE = 1024.0
TOP = 16384.0
H_SCALE = 2.0 ** -20
SLOTS = 4

L_RE, L_IM, P_RE, P_IM, Q_RE, Q_IM, C_RE, C_IM, LOG_STEP, SKIP_D = range(10)

EXP_TERMS = [1.0, 1.0, 1 / 2, 1 / 6, 1 / 24, 1 / 120, 1 / 720, 1 / 5040, 1 / 40320, 1 / 362880]
LN2_HI, LN2_LO = 0.693359375, -2.12194440e-4

(SUM1, NM1, SSQ1, VE1, STD1, R0, T0, T1, SC1, NB1, S2A, S2B, NM2, SSQ2, VE2, STD2, Q0, Q1, Q2, SC2) = range(20)
NSC = 24


def build(nc, ids, table, params, vct, bp, w_in, bw_in, trig, cos_s, dft, tw, ident_in, expert_in, krows, out):
    f32, f16, i32, u32 = mybir.dt.float32, mybir.dt.float16, mybir.dt.int32, mybir.dt.uint32
    ALU, ACT, AX = mybir.AluOpType, mybir.ActivationFunctionType, mybir.AxisListType.X
    V, S, G, PE = nc.vector, nc.scalar, nc.gpsimd, nc.tensor
    RMAX = bass.bass_isa.ReduceOp.max
    KW = 1280

    ctx = ExitStack()
    with ctx:
        def sb(name, shape, dt=f32):
            return ctx.enter_context(nc.sbuf_tensor(name, shape, dt))

        def pb(name, shape, dt=f32):
            return ctx.enter_context(nc.psum_tensor(name, shape, dt))

        def sem(name):
            return ctx.enter_context(nc.semaphore(name))

        ids_raw = sb("ids_raw", [P, NT], i32)
        ids_ok = sb("ids_ok", [P, NT], i32)
        ids_now = sb("ids_now", [P, SLOTS], i32)
        par = sb("par", [P, 10])
        vct_sb = sb("vct_sb", [NS, 2, P])
        bp_sb = sb("bp_sb", [NS, 1])
        trig_sb = sb("trig_sb", [P, 2, 512])
        cos_sb = sb("cos_sb", [P, NB])
        dft_sb = sb("dft_sb", [P, 2, P])
        tw_sb = sb("tw_sb", [16, D])
        ident = sb("ident", [P, P])
        expert = sb("expert", [P, E * R])
        ones = sb("ones", [P, P])
        eps = sb("eps", [P, 1])
        mean_w = sb("mean_w", [P, P])
        w_raw = sb("w_raw", [P, NB, W])
        w_avg = sb("w_avg", [P, W])
        bw_raw = sb("bw_raw", [P, D])
        w_hi = sb("w_hi", [P, NB, W], f16)
        w_lo = sb("w_lo", [P, NB, W], f16)
        bw_hi = sb("bw_hi", [P, D], f16)
        bw_lo = sb("bw_lo", [P, D], f16)
        toe_hi = sb("toe_hi", [P, D], f16)
        toe_lo = sb("toe_lo", [P, D], f16)
        tiny = sb("tiny", [P, 64])
        tiny_i = sb("tiny_i", [P, 2], i32)
        yv = sb("yv", [P, 4])
        v_all = sb("v_all", [P, 8])
        v_mask = sb("v_mask", [P, 2])
        v_er = sb("v_er", [P, 2, 8])
        v_ei = sb("v_ei", [P, 2, 8])
        d_re = sb("d_re", [P, 512])
        d_im = sb("d_im", [P, 512])
        ti = sb("ti", [P, 512])
        sq_re = sb("sq_re", [P, 512])
        sq_im = sb("sq_im", [P, 512])
        den = sb("den", [P, 512])
        inv = sb("inv", [P, 512])
        e_re = sb("e_re", [P, 512])
        e_im = sb("e_im", [P, 512])
        kap = sb("kap", [P, 8, NB])
        fx = sb("fx", [P, 12, 2, NB])
        f_a = sb("f_a", [P, 2, NB])
        f_b = sb("f_b", [P, 2, NB])
        zt = sb("zt", [16, NB, P])
        k_row = sb("k_row", [1, 2, KW], f16)
        cmax = sb("cmax", [P, 4])
        amax = sb("amax", [P, 4])
        scl = sb("scl", [P, 16])
        h0 = sb("h0", [P, SLOTS, D])
        h2 = sb("h2", [P, SLOTS, D])
        u = sb("u", [P, 2, D])
        z = sb("z", [P, 2, D])
        ut_hi = sb("ut_hi", [P, 2, D], f16)
        ut_lo = sb("ut_lo", [P, 2, D], f16)
        zt_hi = sb("zt_hi", [P, D], f16)
        zt_lo = sb("zt_lo", [P, D], f16)
        junk = sb("junk", [P, 3, 2, D], mybir.dt.bfloat16)
        sc = sb("sc", [P, SLOTS, NSC])
        coef = sb("coef", [P, SLOTS])
        top8 = sb("top8", [P, 8])
        arg8 = sb("arg8", [P, 8], u32)
        argf = sb("argf", [P, 1])
        sel = sb("sel", [P, E * R])
        wht_hi = sb("wht_hi", [P, P], f16)
        wht_lo = sb("wht_lo", [P, P], f16)

        y = [pb("y0", [P, D]), pb("y1", [P, D])]
        tr = pb("tr", [P, D])
        hx = pb("hx", [P, 512])
        ff = pb("ff", [P, 512])
        XT = 256

        ld = {n: sem("ld_" + n) for n in ("ids", "par", "vct", "bp", "w", "bw", "trig", "cos", "dft", "tw", "id", "ex")}
        ones_ready, bvec_done, wmean_done = sem("ones_ready"), sem("bvec_done"), sem("wmean_done")
        pre_dve = sem("pre_dve")
        ids_clipped, cos_parts, den_im, squares = sem("ids_clipped"), sem("cos_parts"), sem("den_im"), sem("squares")
        cauchy_in, cauchy_done, spec_ready, z_done = sem("cauchy_in"), sem("cauchy_done"), sem("spec_ready"), sem("z_done")
        zt_ready, k_done, krow_part, krow_stored = sem("zt_ready"), sem("k_done"), sem("krow_part"), sem("krow_stored")
        ld_toe, colmax_ready, max_ready, weights_ready = sem("ld_toe"), sem("colmax_ready"), sem("max_ready"), sem("weights_ready")
        gathered = [sem(f"gathered{k}") for k in range(SLOTS)]
        stored = [sem(f"stored{k}") for k in range(SLOTS)]
        ids_taken = sem("ids_taken")
        dve_passed, pool_passed = sem("dve_passed"), sem("pool_passed")
        sum1_ready, negmean1_ready, ssq1_ready, std1_ready = (
            sem("sum1_ready"), sem("negmean1_ready"), sem("ssq1_ready"), sem("std1_ready"))
        inv1_ready, newton1, scale1_ready, u_ready = sem("inv1_ready"), sem("newton1"), sem("scale1_ready"), sem("u_ready")
        tru_done, uthi_ready, utlo_ready = sem("tru_done"), sem("uthi_ready"), sem("utlo_ready")
        trz_done, zthi_ready, ztlo_ready = sem("trz_done"), sem("zthi_ready"), sem("ztlo_ready")
        conv_half, conv_done = sem("conv_half"), sem("conv_done")
        h2_done, negmean2_ready, ssq2_ready, std2_ready = sem("h2_done"), sem("negmean2_ready"), sem("ssq2_ready"), sem("std2_ready")
        n2a, n2b, n2c, n2d, z_ready = sem("n2a"), sem("n2b"), sem("n2c"), sem("n2d"), sem("z_ready")
        ha_done, top_ready, arg_ready, argf_ready, sel_ready, coef_ready = (
            sem("ha_done"), sem("top_ready"), sem("arg_ready"), sem("argf_ready"), sem("sel_ready"), sem("coef_ready"))
        whtr_done, whthi_ready, whtlo_ready = sem("whtr_done"), sem("whthi_ready"), sem("whtlo_ready")
        ffn_half, ffn_done, final_half, final_done = sem("ffn_half"), sem("ffn_done"), sem("final_half"), sem("final_done")

        block = ctx.enter_context(nc.Block())
        out_t = out.rearrange("(t p) d -> t p d", p=P)

        def slot16(base, off):
            return base * 4 + 16 * (off // SLOTS + 1)

        @block.sync
        def _(sp):
            sp.dma_start(par[:, :], params).then_inc(ld["par"], 16)
            sp.dma_start(trig_sb[:, :, :], trig).then_inc(ld["trig"], 16)
            sp.dma_start(ids_raw[:, :], ids).then_inc(ld["ids"], 16)
            sp.dma_start(w_raw[:, :, :], w_in).then_inc(ld["w"], 16)
            sp.dma_start(dft_sb[:, :, :], dft).then_inc(ld["dft"], 16)
            sp.dma_start(tw_sb[:, :], tw).then_inc(ld["tw"], 16)
            sp.dma_start(ident[:, :], ident_in).then_inc(ld["id"], 16)
            sp.wait_ge(krow_part, 2)
            sp.dma_start(krows[0:1, 0:2 * KW], k_row[0:1, 0:2, :].rearrange("o r x -> o (r x)")).then_inc(krow_stored, 16)
            sp.wait_ge(krow_stored, 16)
            for r, t in enumerate((toe_hi, toe_lo)):
                sp.dma_start(t[:, :], bass.AP(tensor=krows.tensor, offset=r * KW, ap=[[1, P], [1, D]])).then_inc(ld_toe, 16)

            def store(base, off):
                sp.wait_ge(final_done, base + off + 1)
                sp.dma_start(out_t[base + off, :, :], h2[:, off % SLOTS, :]).then_inc(stored[off % SLOTS], 16)

            with sp.Fori(0, NT // SLOTS) as turn:
                first = sp.snap(turn * SLOTS)
                for k in range(SLOTS):
                    store(first, k)
            for k in range(SLOTS):
                sp.wait_ge(stored[k], 16 * (NT // SLOTS + 1))

        @block.gpsimd
        def _(pool):
            for k in range(SLOTS):
                pool.sem_inc(stored[k], 16)
            G.memset(eps[:, :], EPS)
            G.memset(ones[:, :], 1.0)
            G.memset(mean_w[:, :], 1.0 / D)
            G.memset(v_mask[:, :], 0.0)
            G.memset(k_row[:, :, :], 0.0).then_inc(ones_ready, 1)
            pool.wait_ge(ids_clipped, 1)

            def take_ids(base, off):
                k = off % SLOTS
                G.tensor_copy(ids_now[:, k:k + 1], ids_ok[:, bass.ds(base + off, 1)]).then_inc(ids_taken, 1)
                pool.wait_ge(ids_taken, base + off + 1)
                pool.sem_inc(pool_passed, 1)

            def gather(off):
                G.indirect_dma_start(
                    out=h0[:, off % SLOTS, :], out_offset=None, in_=table,
                    in_offset=bass.IndirectOffsetOnAxis(ap=ids_now[:, off % SLOTS:off % SLOTS + 1], axis=0),
                ).then_inc(gathered[off % SLOTS], 16)

            def centre(base, off):
                k = off % SLOTS
                pool.wait_ge(sum1_ready, base + off + 1)
                pool.sem_inc(pool_passed, 1)
                G.tensor_scalar(sc[:, k, NM1:NM1 + 1], sc[:, k, SUM1:SUM1 + 1], -1.0 / D, 1.0,
                                ALU.mult, ALU.mult).then_inc(negmean1_ready, 1)

            def scale1(base, off):
                k, n = off % SLOTS, (base + off) * 4

                def s(j):
                    return sc[:, k, j:j + 1]

                pool.wait_ge(ssq1_ready, base + off + 1)
                pool.sem_inc(pool_passed, 1)
                G.tensor_scalar(s(VE1), s(SSQ1), 1.0 / D, EPS, ALU.mult, ALU.add).then_inc(newton1, 1)
                pool.wait_ge(inv1_ready, base + off + 1)
                pool.sem_inc(pool_passed, 1)
                pool.wait_ge(newton1, n + 1)
                pool.sem_inc(pool_passed, 1)
                G.tensor_scalar(s(T0), s(VE1), s(R0), s(R0), ALU.mult, ALU.mult).then_inc(newton1, 1)
                pool.wait_ge(newton1, n + 2)
                pool.sem_inc(pool_passed, 1)
                G.tensor_scalar(s(T1), s(T0), -0.5, 1.5, ALU.mult, ALU.add).then_inc(newton1, 1)
                pool.wait_ge(newton1, n + 3)
                pool.sem_inc(pool_passed, 1)
                G.tensor_scalar(s(SC1), s(T1), s(R0), U_SCALE, ALU.mult, ALU.mult).then_inc(newton1, 1)
                pool.wait_ge(newton1, n + 4)
                pool.sem_inc(pool_passed, 1)
                G.tensor_scalar(s(NB1), s(NM1), s(SC1), 1.0, ALU.mult, ALU.mult).then_inc(scale1_ready, 1)

            for t in range(SLOTS):
                take_ids(0, t)
                gather(t)
            centre(0, 0)
            centre(0, 1)
            scale1(0, 0)
            scale1(0, 1)
            pool.wait_ge(colmax_ready, 1)
            G.partition_all_reduce(amax[:, 0:2], cmax[:, 0:2], P, RMAX).then_inc(max_ready, 1)

            def step(base, off, fetch=True):
                if fetch:
                    pool.wait_ge(h2_done, base + off - 1)
                    take_ids(base, off + 2)
                    gather(off + 2)
                centre(base, off + 2)
                scale1(base, off + 2)

            step(0, 0, fetch=False)
            step(0, 1, fetch=False)
            with pool.Fori(0, NT // SLOTS - 1) as turn:
                first = pool.snap(turn * SLOTS)
                for k in range(SLOTS):
                    step(first, k + 2)

        @block.scalar
        def _(act):
            act.dma_start(vct_sb[:, :, :], vct).then_inc(ld["vct"], 16)
            act.dma_start(bp_sb[:, :], bp).then_inc(ld["bp"], 16)
            act.dma_start(cos_sb[:, :], cos_s).then_inc(ld["cos"], 16)
            act.dma_start(expert[:, :], expert_in).then_inc(ld["ex"], 16)
            act.dma_start(bw_raw[:, :], bw_in).then_inc(ld["bw"], 16)
            act.wait_ge(ld["par"], 16)
            act.wait_ge(ld["trig"], 16)
            S.activation(ti[:, :], trig_sb[:, 0, :], ACT.Copy, scale=par[:, L_IM:L_IM + 1]).then_inc(cos_parts, 1)
            S.activation(d_re[:, :], trig_sb[:, 0, :], ACT.Copy, scale=par[:, L_RE:L_RE + 1]).then_inc(cos_parts, 1)
            act.wait_ge(cos_parts, 2)
            S.activation(sq_re[:, :], d_re[:, :], ACT.Square).then_inc(squares, 1)
            act.wait_ge(den_im, 1)
            S.activation(sq_im[:, :], d_im[:, :], ACT.Square).then_inc(squares, 1)
            def sum1(base, off):
                k = off % SLOTS
                act.wait_ge(gathered[k], slot16(base, off))
                S.activation(junk[:, 0, off % 2, :], h0[:, k, :], ACT.Copy, accum_out=sc[:, k, SUM1:SUM1 + 1]).then_inc(sum1_ready, 1)

            def ssq1(base, off):
                k = off % SLOTS
                act.wait_ge(negmean1_ready, base + off + 1)
                S.activation(junk[:, 1, off % 2, :], h0[:, k, :], ACT.Square, bias=sc[:, k, NM1:NM1 + 1],
                             accum_out=sc[:, k, SSQ1:SSQ1 + 1]).then_inc(ssq1_ready, 1)
                act.wait_ge(ssq1_ready, base + off + 1)
                S.activation(sc[:, k, STD1:STD1 + 1], sc[:, k, SSQ1:SSQ1 + 1], ACT.Sqrt, bias=eps[:, :],
                             scale=1.0 / D).then_inc(std1_ready, 1)

            def norm1(base, off):
                k = off % SLOTS
                act.wait_ge(scale1_ready, base + off + 1)
                S.activation(u[:, off % 2, :], h0[:, k, ::-1], ACT.Identity, bias=sc[:, k, NB1:NB1 + 1],
                             scale=sc[:, k, SC1:SC1 + 1]).then_inc(u_ready, 1)

            def hi_u(base, off):
                for h in range(2):
                    act.wait_ge(tru_done, (base + off) * 2 + h + 1)
                    S.copy(ut_hi[:, off % 2, 512 * h:512 * h + 512], tr[:, 512 * h:512 * h + 512]).then_inc(uthi_ready, 1)

            def hi_z(base, off):
                for h in range(2):
                    act.wait_ge(trz_done, (base + off) * 2 + h + 1)
                    if h == 0 and (off or base is not 0):
                        act.wait_ge(ha_done, base + off)
                    S.copy(zt_hi[:, 512 * h:512 * h + 512], tr[:, 512 * h:512 * h + 512]).then_inc(zthi_ready, 1)

            def ssq2(base, off):
                k = off % SLOTS
                act.wait_ge(negmean2_ready, base + off + 1)
                S.activation(junk[:, 2, off % 2, :], h2[:, k, :], ACT.Square, bias=sc[:, k, NM2:NM2 + 1],
                             accum_out=sc[:, k, SSQ2:SSQ2 + 1]).then_inc(ssq2_ready, 1)
                act.wait_ge(ssq2_ready, base + off + 1)
                S.activation(sc[:, k, STD2:STD2 + 1], sc[:, k, SSQ2:SSQ2 + 1], ACT.Sqrt, bias=eps[:, :],
                             scale=1.0 / D).then_inc(std2_ready, 1)

            def hi_wh(base, off):
                act.wait_ge(whtr_done, base + off + 1)
                S.mul(wht_hi[:, :], hx[:, XT:XT + P], H_SCALE).then_inc(whthi_ready, 1)

            def step(base, off, one=True, two=True, stage=True, turn=True):
                if one:
                    ssq2(base, off - 1)
                if stage:
                    sum1(base, off + 2)
                if turn:
                    hi_u(base, off + 1)
                if two:
                    hi_wh(base, off - 2)
                if stage:
                    ssq1(base, off + 2)
                if one:
                    hi_z(base, off - 1)
                if stage:
                    norm1(base, off + 2)

            act.wait_ge(ones_ready, 1)
            sum1(0, 0)
            sum1(0, 1)
            ssq1(0, 0)
            ssq1(0, 1)
            norm1(0, 0)
            norm1(0, 1)
            hi_u(0, 0)
            step(0, 0, one=False, two=False)
            step(0, 1, two=False)
            with act.Fori(0, NT // SLOTS - 1) as turn:
                first = act.snap(turn * SLOTS)
                for k in range(SLOTS):
                    step(first, k + 2)
            step(0, NT - 2, stage=False)
            step(0, NT - 1, stage=False, turn=False)
            step(0, NT, stage=False, turn=False)
            step(0, NT + 1, one=False, stage=False, turn=False)

        @block.vector
        def _(dve):
            steps = [0]

            def link(ins):
                steps[0] += 1
                ins.then_inc(pre_dve, 1)
                dve.wait_ge(pre_dve, steps[0])

            def c(j, n=1):
                return tiny[:, j:j + n]

            dve.wait_ge(ld["ids"], 16)
            V.tensor_scalar(ids_ok[:, :], ids_raw[:, :], 0, VOCAB - 1, ALU.max, ALU.min).then_inc(ids_clipped, 1)
            dve.wait_ge(ld["par"], 16)
            link(V.tensor_scalar(c(0), par[:, LOG_STEP:LOG_STEP + 1], -1.0, 87.0, ALU.mult, ALU.min))
            link(V.tensor_scalar(c(0), c(0), -87.0, None, ALU.max))
            link(V.tensor_scalar(tiny_i[:, 0:1], c(0), 1.4426950408889634, None, ALU.mult))
            link(V.tensor_copy(c(1), tiny_i[:, 0:1]))
            link(V.scalar_tensor_tensor(c(2), c(1), -LN2_HI, c(0), ALU.mult, ALU.add))
            link(V.scalar_tensor_tensor(c(2), c(1), -LN2_LO, c(2), ALU.mult, ALU.add))
            V.memset(c(3), EXP_TERMS[-1])
            link(V.tensor_scalar(tiny_i[:, 0:1], c(1), 128.0, None, ALU.add))
            link(V.tensor_scalar(tiny_i[:, 1:2], tiny_i[:, 0:1], 23, None, ALU.logical_shift_left))
            for term in EXP_TERMS[-2::-1]:
                link(V.tensor_scalar(c(3), c(3), c(2), term, ALU.mult, ALU.add))
            link(V.tensor_tensor(c(4), c(3), tiny_i[:, 1:2].bitcast(f32), ALU.mult))
            dve.wait_ge(cos_parts, 1)
            V.scalar_tensor_tensor(d_im[:, :], trig_sb[:, 1, :], c(4), ti[:, :], ALU.mult, ALU.subtract).then_inc(den_im, 1)
            dve.wait_ge(ones_ready, 1)
            V.memset(v_mask[0:64, 0:1], 1.0)
            V.memset(v_mask[64:128, 1:2], 1.0)
            V.tensor_copy(yv[:, 1:4:2], par[:, P_RE:P_IM + 1])
            dve.wait_ge(bvec_done, 1)
            link(V.tensor_copy(yv[:, 0:3:2], hx[:, 0:2]))
            for i, (re, im) in enumerate(((C_RE, C_IM), (Q_RE, Q_IM))):
                xr, xi = par[:, re:re + 1], par[:, im:im + 1]
                V.tensor_scalar(c(8 + 4 * i, 2), yv[:, 2:4], xi, None, ALU.mult)
                link(V.tensor_scalar(c(10 + 4 * i, 2), yv[:, 0:2], xi, None, ALU.mult))
                V.scalar_tensor_tensor(v_all[:, 2 * i:2 * i + 2], yv[:, 0:2], xr, c(8 + 4 * i, 2), ALU.mult, ALU.add)
                link(V.scalar_tensor_tensor(v_all[:, 4 + 2 * i:6 + 2 * i], yv[:, 2:4], xr, c(10 + 4 * i, 2), ALU.mult, ALU.subtract))
            for h in range(2):
                m = v_mask[:, h:h + 1]
                V.tensor_scalar(v_er[:, h, :], v_all[:, :], m, None, ALU.mult)
                V.tensor_scalar(v_ei[:, h, 0:4], v_all[:, 4:8], m, None, ALU.mult)
                last = V.tensor_scalar(v_ei[:, h, 4:8], v_all[:, 0:4], m, -1.0, ALU.mult, ALU.mult)
            link(last)
            dve.wait_ge(squares, 2)
            link(V.tensor_tensor(den[:, :], sq_re[:, :], sq_im[:, :], ALU.add))
            link(V.reciprocal(inv[:, :], den[:, :]))
            V.scalar_tensor_tensor(e_re[:, :], d_re[:, :], -1.0, inv[:, :], ALU.mult, ALU.mult)
            V.tensor_tensor(e_im[:, :], d_im[:, :], inv[:, :], ALU.mult).then_inc(cauchy_in, 1)
            dve.wait_ge(wmean_done, 1)
            dve.wait_ge(ld["w"], 16)
            link(V.tensor_copy(w_avg[:, :], ff[:, 0:W]))
            link(V.tensor_tensor(w_raw[:, :, :], w_raw[:, :, :],
                                 w_avg[:, :].rearrange("p (o w) -> p o w", o=1).broadcast_to([P, NB, W]), ALU.subtract))
            V.tensor_reduce(cmax[:, 0:1], w_raw[:, :, :].rearrange("p b w -> p (b w)"), AX, ALU.max, apply_absolute_value=True)
            dve.wait_ge(ld["bw"], 16)
            V.tensor_reduce(cmax[:, 1:2], bw_raw[:, :], AX, ALU.max, apply_absolute_value=True).then_inc(colmax_ready, 1)
            dve.wait_ge(cauchy_done, 1)
            link(V.tensor_copy(kap[:, :, :], y[0][:, 0:64].rearrange("p (f c) -> p c f", c=8)))
            dve.wait_ge(ld["cos"], 16)

            def pair(j):
                return kap[:, j:j + 5:4, :]

            def both(x):
                return x.rearrange("p (o f) -> p o f", o=1).broadcast_to([P, 2, NB])

            cosb = both(cos_sb[:, :])
            V.tensor_tensor(fx[:, 0, :, :], pair(1), both(kap[:, 2, :]), ALU.mult)
            V.tensor_tensor(fx[:, 1, :, :], pair(1), both(kap[:, 6, :]), ALU.mult)
            link(V.tensor_tensor(fx[:, 2, :, :], pair(3), cosb, ALU.mult))
            V.tensor_tensor(fx[:, 3, 0, :], fx[:, 0, 0, :], fx[:, 1, 1, :], ALU.subtract)
            V.tensor_tensor(fx[:, 3, 1, :], fx[:, 0, 1, :], fx[:, 1, 0, :], ALU.add)
            link(V.tensor_scalar(fx[:, 2, 0, :], fx[:, 2, 0, :], 1.0, None, ALU.add))
            V.tensor_tensor(fx[:, 5, :, :], fx[:, 2, :, :], fx[:, 2, :, :], ALU.mult)
            link(V.tensor_tensor(fx[:, 4, :, :], fx[:, 3, :, :], cosb, ALU.mult))
            V.tensor_tensor(fx[:, 6, 0, :], fx[:, 5, 0, :], fx[:, 5, 1, :], ALU.add)
            V.tensor_tensor(fx[:, 7, :, :], fx[:, 4, :, :], both(fx[:, 2, 0, :]), ALU.mult)
            link(V.tensor_tensor(fx[:, 8, :, :], fx[:, 4, :, :], both(fx[:, 2, 1, :]), ALU.mult))
            V.reciprocal(fx[:, 6, 1, :], fx[:, 6, 0, :])
            V.tensor_tensor(fx[:, 9, 0, :], fx[:, 7, 0, :], fx[:, 8, 1, :], ALU.add)
            link(V.tensor_tensor(fx[:, 9, 1, :], fx[:, 7, 1, :], fx[:, 8, 0, :], ALU.subtract))
            link(V.tensor_tensor(fx[:, 10, :, :], fx[:, 9, :, :], both(fx[:, 6, 1, :]), ALU.mult))
            link(V.tensor_tensor(f_a[:, :, :], pair(0), fx[:, 10, :, :], ALU.subtract))
            V.tensor_scalar(f_b[:, 0, :], f_a[:, 1, :], -1.0, None, ALU.mult)
            V.tensor_copy(f_b[:, 1, :], f_a[:, 0, :]).then_inc(spec_ready, 1)
            dve.wait_ge(z_done, 1)
            dve.wait_ge(ld["tw"], 16)
            V.tensor_tensor(zt[:, :, :], tw_sb[:, :].rearrange("q (a b) -> q a b", b=P),
                            y[0][0:16, 512:640].rearrange("q (o b) -> q o b", o=1).broadcast_to([16, NB, P]),
                            ALU.mult).then_inc(zt_ready, 1)
            dve.wait_ge(k_done, 1)
            link(V.tensor_reduce(scl[:, 0:1], y[1][:, :], AX, ALU.max, apply_absolute_value=True))
            link(V.tensor_scalar(scl[:, 1:2], scl[:, 0:1], 1e-30, 1.0 / TOP, ALU.max, ALU.mult))
            link(V.reciprocal(scl[:, 2:3], scl[:, 1:2]))
            dve.wait_ge(ones_ready, 1)
            V.tensor_scalar(k_row[0:1, 0, P - 1:P - 1 + D], y[1][0:1, :], scl[0:1, 2:3], None, ALU.mult).then_inc(krow_part, 1)
            dve.wait_ge(krow_part, 1)
            V.scalar_tensor_tensor(k_row[0:1, 1, P - 1:P - 1 + D], y[1][0:1, :], scl[0:1, 2:3],
                                   k_row[0:1, 0, P - 1:P - 1 + D], ALU.mult, ALU.subtract).then_inc(krow_part, 1)

            def inv1(base, off):
                k = off % SLOTS
                dve.wait_ge(std1_ready, base + off + 1)
                V.reciprocal(sc[:, k, R0:R0 + 1], sc[:, k, STD1:STD1 + 1]).then_inc(inv1_ready, 1)

            def lo_u(base, off):
                for h in range(2):
                    a = 512 * h
                    dve.wait_ge(uthi_ready, (base + off) * 2 + h + 1)
                    V.tensor_tensor(ut_lo[:, off % 2, a:a + 512], tr[:, a:a + 512], ut_hi[:, off % 2, a:a + 512],
                                    ALU.subtract).then_inc(utlo_ready, 1)

            def lo_z(base, off):
                for h in range(2):
                    a = 512 * h
                    dve.wait_ge(zthi_ready, (base + off) * 2 + h + 1)
                    V.tensor_tensor(zt_lo[:, a:a + 512], tr[:, a:a + 512], zt_hi[:, a:a + 512],
                                    ALU.subtract).then_inc(ztlo_ready, 1)

            inv1(0, 0)
            inv1(0, 1)
            lo_u(0, 0)
            dve.wait_ge(max_ready, 1)
            link(V.tensor_scalar(scl[:, 3:5], amax[:, 0:2], 1e-30, 1.0 / TOP, ALU.max, ALU.mult))
            link(V.reciprocal(scl[:, 5:7], scl[:, 3:5]))
            link(V.tensor_scalar(w_raw[:, :, :], w_raw[:, :, :], scl[:, 5:6], None, ALU.mult))
            link(V.tensor_copy(w_hi[:, :, :], w_raw[:, :, :]))
            link(V.tensor_tensor(w_lo[:, :, :], w_raw[:, :, :], w_hi[:, :, :], ALU.subtract))
            link(V.tensor_scalar(bw_raw[:, :], bw_raw[:, :], scl[:, 6:7], None, ALU.mult))
            link(V.tensor_copy(bw_hi[:, :], bw_raw[:, :]))
            V.tensor_tensor(bw_lo[:, :], bw_raw[:, :], bw_hi[:, :], ALU.subtract).then_inc(weights_ready, 1)
            V.tensor_scalar(scl[:, 7:8], scl[:, 1:2], 1.0 / U_SCALE, None, ALU.mult)
            link(V.tensor_tensor(scl[:, 8:9], scl[:, 3:4], scl[:, 4:5], ALU.mult))

            def residual(base, off, half):
                k, a = off % SLOTS, 512 * half
                if half:
                    dve.wait_ge(conv_done, base + off + 1)
                else:
                    dve.wait_ge(conv_half, base + off + 1)
                    dve.wait_ge(stored[k], slot16(base, off))
                last = V.scalar_tensor_tensor(h2[:, k, a:a + 512], y[off % 2][:, a:a + 512], scl[:, 7:8],
                                              h0[:, k, a:a + 512], ALU.mult, ALU.add,
                                              accum_out=sc[:, k, S2A + half:S2A + half + 1])
                if half:
                    last.then_inc(h2_done, 1)
                    dve.wait_ge(h2_done, base + off + 1)
                    V.tensor_scalar(sc[:, k, NM2:NM2 + 1], sc[:, k, S2A:S2A + 1], sc[:, k, S2B:S2B + 1], -1.0 / D,
                                    ALU.add, ALU.mult).then_inc(negmean2_ready, 1)

            def norm2(base, off):
                k, n = off % SLOTS, base + off + 1

                def s(j):
                    return sc[:, k, j:j + 1]

                dve.wait_ge(ssq2_ready, n)
                V.tensor_scalar(s(VE2), s(SSQ2), 1.0 / D, EPS, ALU.mult, ALU.add)
                dve.wait_ge(std2_ready, n)
                V.reciprocal(s(Q0), s(STD2)).then_inc(n2a, 1)
                dve.wait_ge(n2a, n)
                V.tensor_scalar(s(Q1), s(VE2), s(Q0), s(Q0), ALU.mult, ALU.mult).then_inc(n2b, 1)
                dve.wait_ge(n2b, n)
                V.tensor_scalar(s(Q2), s(Q1), -0.5, 1.5, ALU.mult, ALU.add).then_inc(n2c, 1)
                dve.wait_ge(n2c, n)
                V.tensor_scalar(s(SC2), s(Q2), s(Q0), U_SCALE, ALU.mult, ALU.mult).then_inc(n2d, 1)
                dve.wait_ge(n2d, n)
                V.tensor_scalar(z[:, off % 2, :], h2[:, k, :], s(NM2), s(SC2), ALU.add, ALU.mult).then_inc(z_ready, 1)

            def route(base, off):
                k, n = off % SLOTS, base + off + 1
                dve.wait_ge(ha_done, n)
                dve.sem_inc(dve_passed, 1)
                V.max(top8[:, :], hx[:, 0:E]).then_inc(top_ready, 1)
                dve.wait_ge(top_ready, n)
                dve.sem_inc(dve_passed, 1)
                V.max_index(arg8[:, :], top8[:, :], hx[:, 0:E]).then_inc(arg_ready, 1)
                dve.wait_ge(arg_ready, n)
                V.tensor_copy(argf[:, :], arg8[:, 0:1]).then_inc(argf_ready, 1)
                dve.wait_ge(argf_ready, n)
                V.scalar_tensor_tensor(sel[:, :], expert[:, :], argf[:, :], hx[:, E:W],
                                       ALU.is_equal, ALU.mult).then_inc(sel_ready, 1)
                V.tensor_scalar(coef[:, k:k + 1], top8[:, 0:1], scl[:, 3:4], scl[:, 8:9],
                                ALU.mult, ALU.mult).then_inc(coef_ready, 1)

            def lo_wh(base, off):
                dve.wait_ge(whthi_ready, base + off + 1)
                V.scalar_tensor_tensor(wht_lo[:, :], hx[:, XT:XT + P], H_SCALE, wht_hi[:, :],
                                       ALU.mult, ALU.subtract).then_inc(whtlo_ready, 1)

            def final(base, off, half):
                k, n, a = off % SLOTS, base + off + 1, 512 * half
                dve.wait_ge(ffn_done if half else ffn_half, n)
                if not half:
                    dve.wait_ge(coef_ready, n)
                V.scalar_tensor_tensor(h2[:, k, a:a + 512], ff[:, :], coef[:, k:k + 1], h2[:, k, a:a + 512],
                                       ALU.mult, ALU.add).then_inc(final_done if half else final_half, 1)

            def step(base, off, one=True, two=True, stage=True, turn=True, own=True):
                if two:
                    route(base, off - 2)
                if one:
                    norm2(base, off - 1)
                if turn:
                    lo_u(base, off + 1)
                if two:
                    lo_wh(base, off - 2)
                if stage:
                    inv1(base, off + 2)
                if one:
                    lo_z(base, off - 1)
                if two:
                    final(base, off - 2, 0)
                if own:
                    residual(base, off, 0)
                if two:
                    final(base, off - 2, 1)
                if own:
                    residual(base, off, 1)

            dve.wait_ge(ld["ex"], 16)
            step(0, 0, one=False, two=False)
            step(0, 1, two=False)
            with dve.Fori(0, NT // SLOTS - 1) as turn:
                first = dve.snap(turn * SLOTS)
                for k in range(SLOTS):
                    step(first, k + 2)
            step(0, NT - 2, stage=False)
            step(0, NT - 1, stage=False, turn=False)
            step(0, NT, stage=False, turn=False, own=False)
            step(0, NT + 1, one=False, stage=False, turn=False, own=False)

        @block.tensor
        def _(pe):
            pe.wait_ge(ld["vct"], 16)
            pe.wait_ge(ld["bp"], 16)
            for c in range(2):
                last = PE.matmul(hx[:, c:c + 1], vct_sb[:, c, :], bp_sb[:, :], start=True, stop=True)
            last.then_inc(bvec_done, 1)
            pe.wait_ge(ld["w"], 16)
            pe.wait_ge(ones_ready, 1)
            for b in range(NB):
                last = PE.matmul(ff[:, 0:W], mean_w[:, :], w_raw[:, b, :], start=(b == 0), stop=(b == NB - 1))
            last.then_inc(wmean_done, 1)
            pe.wait_ge(cauchy_in, 1)
            for g in range(4):
                o = y[0][:, 16 * g:16 * g + 16]
                PE.matmul(o, e_re[:, P * g:P * g + P], v_er[:, :, :].rearrange("p h c -> p (h c)"), start=True, stop=False)
                last = PE.matmul(o, e_im[:, P * g:P * g + P], v_ei[:, :, :].rearrange("p h c -> p (h c)"), start=False, stop=True)
            last.then_inc(cauchy_done, 1)
            pe.wait_ge(spec_ready, 1)
            pe.wait_ge(ld["dft"], 16)
            PE.matmul(y[0][0:16, 512:640], f_a[:, :, :].rearrange("p a f -> p (a f)"), dft_sb[:, 0, :], start=True, stop=False)
            PE.matmul(y[0][0:16, 512:640], f_b[:, :, :].rearrange("p a f -> p (a f)"), dft_sb[:, 1, :],
                      start=False, stop=True).then_inc(z_done, 1)
            pe.wait_ge(zt_ready, 1)
            ztf = zt[:, :, :].rearrange("q a b -> q (a b)")
            for a in (512, 0):
                PE.matmul(y[1][:, a:a + 512], ones[0:16, :], ztf[:, a:a + 512], start=True, stop=True,
                          skip_group_check=True)
            PE.matmul(y[1][:, 0:1], ones[0:1, :], par[0:1, SKIP_D:SKIP_D + 1], start=False, stop=True,
                      skip_group_check=True).then_inc(k_done, 1)

            def transposes(base, off, rows, ready, free, freed, done):
                pe.wait_ge(ready, base + off + 1)
                for b in range(NB):
                    if free is not None and b % 4 == 0:
                        pe.wait_ge(free, freed + b // 4)
                    last = PE.transpose(tr[:, b * P:(b + 1) * P], rows[:, off % 2, b * P:(b + 1) * P], ident[:, :])
                    if b % 4 == 3:
                        last.then_inc(done, 1)

            def conv(off, jb):
                x = D - (jb + 1) * P
                for part, toe, first in ((ut_hi, toe_hi, jb == 0), (ut_hi, toe_lo, False), (ut_lo, toe_hi, False)):
                    for a in (0, 512):
                        a0 = max(a, jb * P)
                        if a0 < a + 512:
                            last = PE.matmul(y[off % 2][:, a0:a + 512], part[:, off % 2, x:x + P],
                                             toe[:, a0 - jb * P:a + 512 - jb * P], start=first, stop=False,
                                             skip_group_check=True)
                return last

            def experts_in(base, off):
                pe.wait_ge(ztlo_ready, (base + off) * 2 + 2)
                for b in range(NB):
                    for i, (part, w) in enumerate(((zt_hi, w_hi), (zt_hi, w_lo), (zt_lo, w_hi))):
                        last = PE.matmul(hx[:, 0:W], part[:, b * P:(b + 1) * P], w[:, b, :],
                                         start=(b == 0 and i == 0), stop=(b == NB - 1 and i == 2))
                last.then_inc(ha_done, 1)

            def transpose_wh(base, off):
                pe.wait_ge(sel_ready, base + off + 1)
                PE.transpose(hx[:, XT:XT + P], sel[:, :], ident[:, :]).then_inc(whtr_done, 1)

            def experts_out(base, off, half):
                a = 512 * half
                if half:
                    pe.wait_ge(final_half, base + off + 1)
                else:
                    pe.wait_ge(whtlo_ready, base + off + 1)
                    if off or base is not 0:
                        pe.wait_ge(final_done, base + off)
                for i, (part, bw) in enumerate(((wht_hi, bw_hi), (wht_hi, bw_lo), (wht_lo, bw_hi))):
                    last = PE.matmul(ff[:, :], part[:, :], bw[:, a:a + 512], start=(i == 0), stop=(i == 2))
                last.then_inc(ffn_done if half else ffn_half, 1)

            def step(base, off, one=True, two=True, turn=True, own=True):
                if own:
                    pe.wait_ge(utlo_ready, (base + off) * 2 + 2)
                    if off > 1 or base is not 0:
                        pe.wait_ge(h2_done, base + (off - 1))
                    conv(off, 0)
                if turn:
                    if off == 0:
                        transposes(base, off + 1, u, u_ready, utlo_ready, 1, tru_done)
                    elif off == 1 and base is 0:
                        transposes(base, off + 1, u, u_ready, utlo_ready, 3, tru_done)
                    else:
                        transposes(base, off + 1, u, u_ready, ztlo_ready, (base + off - 2) * 2 + 1, tru_done)
                if own:
                    conv(off, 1)
                if two:
                    transpose_wh(base, off - 2)
                if own:
                    conv(off, 2)
                if one:
                    if turn:
                        transposes(base, off - 1, z, z_ready, utlo_ready, (base + off + 1) * 2 + 1, trz_done)
                    else:
                        transposes(base, off - 1, z, z_ready, ztlo_ready, (base + off - 2) * 2 + 1, trz_done)
                if own:
                    conv(off, 3).then_inc(conv_half, 1)
                if two:
                    experts_out(base, off - 2, 0)
                if own:
                    conv(off, 4)
                    conv(off, 5)
                if two:
                    experts_out(base, off - 2, 1)
                if own:
                    conv(off, 6)
                    conv(off, 7).then_inc(conv_done, 1)
                if one:
                    experts_in(base, off - 1)

            pe.wait_ge(ld["id"], 16)
            transposes(0, 0, u, u_ready, None, 0, tru_done)
            pe.wait_ge(ld_toe, 32)
            step(0, 0, one=False, two=False)
            pe.wait_ge(weights_ready, 1)
            step(0, 1, two=False)
            with pe.Fori(0, NT // SLOTS - 1) as turn:
                first = pe.snap(turn * SLOTS)
                for k in range(SLOTS):
                    step(first, k + 2)
            step(0, NT - 2)
            step(0, NT - 1, turn=False)
            step(0, NT, turn=False, own=False)
            step(0, NT + 1, one=False, turn=False, own=False)


def constants():
    lp = np.arange(P, dtype=np.float64)
    res = np.array([4 * h + g for g in range(4) for h in range(2)], dtype=np.float64)
    half = np.arange(P) // NS
    bins = 8 * lp[None, None, :] + 4 * half[:, None, None] + np.arange(4)[None, :, None]
    phi = np.pi * bins / D
    cosphi = np.where(bins == D // 2, 0.0, np.cos(phi))
    trig = np.stack([cosphi.reshape(P, 512), np.sin(phi).reshape(P, 512)], 1)
    b2 = 8 * lp[:, None] + res[None, :]
    cos_s = np.where(b2 == D // 2, 0.0, np.cos(np.pi * b2 / D))
    t1 = np.arange(P)
    ang = np.pi * ((lp[:, None].astype(np.int64) * (2 * t1[None, :] + 1)) % 256) / 128
    dft = np.stack([np.cos(ang), np.sin(ang)], 1)
    t = np.arange(D)
    th = np.pi * ((res[:, None].astype(np.int64) * (2 * t[None, :] + 1)) % (2 * D)) / D
    tw = np.concatenate([np.cos(th), -np.sin(th)], 0) / D
    expert = np.broadcast_to(np.arange(E * R) // R, (P, E * R))
    f = np.float32
    return trig.astype(f), cos_s.astype(f), dft.astype(f), tw.astype(f), np.eye(P, dtype=f), expert.astype(f)


def kernel(x, L0_tok_orig_emb_w, L0_tok_new_emb, L0_attn_Lambda_ri, L0_attn_p_ri, L0_attn_q_ri, L0_attn_Vc_ri,
           L0_attn_Ct_ri, L0_attn_Bp, L0_attn_D, L0_attn_log_step, L0_ffn_route_w, L0_ffn_A, L0_ffn_Bw):
    import concourse.bacc as bacc
    from concourse.bass_utils import run_bass_kernel_spmd

    def a(v):
        return np.asarray(v)

    trig, cos_s, dft, tw, ident, expert = constants()
    lam, p, q, ct = (a(v).reshape(NS, 2) for v in (L0_attn_Lambda_ri, L0_attn_p_ri, L0_attn_q_ri, L0_attn_Ct_ri))
    cols = np.concatenate([lam, p, q, ct], 1)
    ends = np.broadcast_to(np.stack([a(L0_attn_log_step)[0], a(L0_attn_D)[0]]), (P, 2))
    params = np.concatenate([np.concatenate([cols, cols], 0), ends], 1)
    vct = a(L0_attn_Vc_ri).transpose(1, 2, 0)
    w = np.concatenate([a(L0_ffn_route_w).T, a(L0_ffn_A).reshape(E * R, D).T], 1)
    arrays = {
        "ids": a(x).reshape(NT, P).T,
        "table": np.concatenate([a(L0_tok_orig_emb_w), a(L0_tok_new_emb)], 0),
        "params": params,
        "vct": np.concatenate([vct, vct], 2),
        "bp": a(L0_attn_Bp),
        "w": w.reshape(NB, P, W).transpose(1, 0, 2),
        "bw": a(L0_ffn_Bw).transpose(0, 2, 1).reshape(E * R, D),
        "trig": trig, "cos_s": cos_s, "dft": dft, "tw": tw, "ident": ident, "expert": expert,
    }
    arrays = {f"in_{n}": np.ascontiguousarray(v) for n, v in arrays.items()}
    nc = bacc.Bacc("TRN2", target_bir_lowering=False, num_devices=1)
    args = [nc.dram_tensor(n, v.shape, mybir.dt.from_np(v.dtype), kind="ExternalInput").ap() for n, v in arrays.items()]
    krows = nc.dram_tensor("krows", (1, 2 * 1280), mybir.dt.float16, kind="Internal").ap()
    out = nc.dram_tensor("out_rows", (TOK, D), mybir.dt.float32, kind="ExternalOutput").ap()
    build(nc, *args, krows, out)
    r = run_bass_kernel_spmd(nc, [arrays], core_ids=[0])
    return r.results[0]["out_rows"].reshape(8, 512, D)
```

```python
from contextlib import ExitStack

import numpy as np

import concourse.bass as bass
from concourse import mybir

P = 128
TOK = 4096
D = 1024
VOCAB = 8192
NB = D // P
NT = TOK // P
E = 8
R = 16
W = E + E * R
NS = 64
EPS = 1e-5
U_SCALE = 1024.0
TOP = 16384.0
H_SCALE = 2.0 ** -20
SLOTS = 4

L_RE, L_IM, P_RE, P_IM, Q_RE, Q_IM, C_RE, C_IM, LOG_STEP, SKIP_D = range(10)

EXP_TERMS = [1.0, 1.0, 1 / 2, 1 / 6, 1 / 24, 1 / 120, 1 / 720, 1 / 5040]
LN2_HI, LN2_LO = 0.693359375, -2.12194440e-4
LOG2E, MAGIC = 1.4426950408889634, 12583040.0

(SUM1, NM1, SSQ1, VE1, STD1, R0, T0, T1, SC1, NB1, S2A, S2B, NM2, SSQ2, VE2, STD2, Q0, Q1, Q2, SC2) = range(20)
NSC = 24


def build(nc, ids, table, params, vct, bp, w_in, bw_in, trig, cos_s, dft, tw, dft8, ident_in, expert_in, krows, out):
    f32, f16, i32, u32 = mybir.dt.float32, mybir.dt.float16, mybir.dt.int32, mybir.dt.uint32
    ALU, ACT, AX = mybir.AluOpType, mybir.ActivationFunctionType, mybir.AxisListType.X
    V, S, G, PE = nc.vector, nc.scalar, nc.gpsimd, nc.tensor
    RMAX = bass.bass_isa.ReduceOp.max
    KW = P + 2 * D

    ctx = ExitStack()
    with ctx:
        def sb(name, shape, dt=f32):
            return ctx.enter_context(nc.sbuf_tensor(name, shape, dt))

        def pb(name, shape, dt=f32):
            return ctx.enter_context(nc.psum_tensor(name, shape, dt))

        def sem(name):
            return ctx.enter_context(nc.semaphore(name))

        ids_raw = sb("ids_raw", [P, NT], i32)
        ids_ok = sb("ids_ok", [P, NT], i32)
        ids_now = sb("ids_now", [P, SLOTS], i32)
        par = sb("par", [P, 10])
        vct_sb = sb("vct_sb", [NS, 2, P])
        bp_sb = sb("bp_sb", [NS, 1])
        trig_sb = sb("trig_sb", [P, 2, 512])
        cos_sb = sb("cos_sb", [P, NB])
        dft_sb = sb("dft_sb", [P, 2, 2 * P])
        tw_sb = sb("tw_sb", [16, 2 * P])
        dft8_sb = sb("dft8_sb", [16, 4 * NB])
        ident = sb("ident", [P, P])
        expert = sb("expert", [P, E * R])
        ones = sb("ones", [P, P])
        eps = sb("eps", [P, 1])
        mean_w = sb("mean_w", [P, P])
        w_raw = sb("w_raw", [P, NB, W])
        w_avg = sb("w_avg", [P, W])
        bw_raw = sb("bw_raw", [P, D])
        w_hi = sb("w_hi", [P, NB, W], f16)
        w_lo = sb("w_lo", [P, NB, W], f16)
        bw_hi = sb("bw_hi", [P, D], f16)
        bw_lo = sb("bw_lo", [P, D], f16)
        toe_hi = sb("toe_hi", [P, 768], f16)
        toe_lo = sb("toe_lo", [P, 768], f16)
        dif_hi = sb("dif_hi", [P, D], f16)
        dif_lo = sb("dif_lo", [P, D], f16)
        tiny = sb("tiny", [P, 64])
        tiny_i = sb("tiny_i", [P, 1], i32)
        yv = sb("yv", [P, 4])
        v_all = sb("v_all", [P, 8])
        v_mask = sb("v_mask", [P, 2])
        v_er = sb("v_er", [P, 2, 8])
        v_ei = sb("v_ei", [P, 2, 8])
        d_re = sb("d_re", [P, 512])
        d_im = sb("d_im", [P, 512])
        ti = sb("ti", [P, 512])
        sq_re = sb("sq_re", [P, 512])
        sq_im = sb("sq_im", [P, 512])
        den = sb("den", [P, 512])
        inv = sb("inv", [P, 512])
        e_re = sb("e_re", [P, 512])
        e_im = sb("e_im", [P, 512])
        kap = sb("kap", [P, 8, NB])
        fx = sb("fx", [P, 12, 2, NB])
        f_a = sb("f_a", [P, 2, NB])
        f_b = sb("f_b", [P, 2, NB])
        zp = sb("zp", [16, 2 * P])
        zt = sb("zt", [16, P])
        warm = sb("warm", [P, 1])
        k_zero = sb("k_zero", [P, 2 * KW // P], f16)
        k_parts = sb("k_parts", [2 * NB, 2, P], f16)
        cmax = sb("cmax", [P, 4])
        amax = sb("amax", [P, 4])
        scl = sb("scl", [P, 16])
        h0 = sb("h0", [P, SLOTS, D])
        h2 = sb("h2", [P, SLOTS, D])
        u = sb("u", [P, 2, D])
        z = sb("z", [P, 2, D])
        ut_hi = sb("ut_hi", [P, 2, D], f16)
        ut_lo = sb("ut_lo", [P, 2, D], f16)
        u_sum = sb("u_sum", [P, 2, 256])
        x0_sb = sb("x0_sb", [P, 2, 256])
        us_hi = sb("us_hi", [P, 2, 256], f16)
        us_lo = sb("us_lo", [P, 2, 256], f16)
        shared = sb("shared", [P, 2, 256])
        zt_hi = sb("zt_hi", [P, D], f16)
        zt_lo = sb("zt_lo", [P, D], f16)
        junk = sb("junk", [P, 3, 2, D], mybir.dt.bfloat16)
        sc = sb("sc", [P, SLOTS, NSC])
        coef = sb("coef", [P, SLOTS])
        top8 = sb("top8", [P, 8])
        arg8 = sb("arg8", [P, 8], u32)
        argf = sb("argf", [P, 1])
        sel = sb("sel", [P, E * R])
        wht_hi = sb("wht_hi", [P, P], f16)
        wht_lo = sb("wht_lo", [P, P], f16)

        y = [pb("y0", [P, D]), pb("y1", [P, D])]
        tr = pb("tr", [P, D])
        hx = pb("hx", [P, 512])
        ff = pb("ff", [P, 512])
        SH = 256

        ld = {n: sem("ld_" + n) for n in ("ids", "par", "vct", "bp", "w", "bw", "trig", "sin", "cos", "dft", "tw", "d8", "id", "ex")}
        ones_ready, bvec_done, wmean_done = sem("ones_ready"), sem("bvec_done"), sem("wmean_done")
        pre_dve = sem("pre_dve")
        ids_clipped, cos_parts, den_im, squares = sem("ids_clipped"), sem("cos_parts"), sem("den_im"), sem("squares")
        cauchy_in = [sem("cauchy_in0"), sem("cauchy_in1")]
        cauchy_done, spec_ready, z_done = sem("cauchy_done"), sem("spec_ready"), sem("z_done")
        zt_ready, k_done, krow_part, krow_stored = sem("zt_ready"), sem("k_done"), sem("krow_part"), (sem("krow_stored0"), sem("krow_stored1"))
        v_ready, inv_ready, k_cleared, k_sum = sem("v_ready"), sem("inv_ready"), sem("k_cleared"), sem("k_sum")
        ld_toe_hi, ld_toe_lo, ld_rest, ld_dif = sem("ld_toe_hi"), sem("ld_toe_lo"), sem("ld_rest"), sem("ld_dif")
        k_bound, wscale_ready, whi_ready = sem("k_bound"), sem("wscale_ready"), sem("whi_ready")
        colmax_ready, max_ready, weights_ready = sem("colmax_ready"), sem("max_ready"), sem("weights_ready")
        gathered = [sem(f"gathered{k}") for k in range(SLOTS)]
        stored = [sem(f"stored{k}") for k in range(SLOTS)]
        ids_taken = sem("ids_taken")
        dve_passed, pool_passed = sem("dve_passed"), sem("pool_passed")
        sum1_ready, negmean1_ready, ssq1_ready, std1_ready = (
            sem("sum1_ready"), sem("negmean1_ready"), sem("ssq1_ready"), sem("std1_ready"))
        inv1_ready, newton1, scale1_ready, u_ready = sem("inv1_ready"), sem("newton1"), sem("scale1_ready"), sem("u_ready")
        tru_done, uthi_ready, utlo_ready = sem("tru_done"), sem("uthi_ready"), sem("utlo_ready")
        trz_done, zthi_ready, ztlo_ready = sem("trz_done"), sem("zthi_ready"), sem("ztlo_ready")
        x0_ready, usum_ready, ushi_ready, us_ready = sem("x0_ready"), sem("usum_ready"), sem("ushi_ready"), sem("us_ready")
        share_done, share_out, shared_in = sem("share_done"), sem("share_out"), sem("shared_in")
        conv_half, conv_done = sem("conv_half"), sem("conv_done")
        h2_done, negmean2_ready, ssq2_ready, std2_ready = sem("h2_done"), sem("negmean2_ready"), sem("ssq2_ready"), sem("std2_ready")
        n2a, n2b, n2c, n2d, z_ready = sem("n2a"), sem("n2b"), sem("n2c"), sem("n2d"), sem("z_ready")
        ha_done, top_ready, arg_ready, argf_ready, sel_ready, coef_ready = (
            sem("ha_done"), sem("top_ready"), sem("arg_ready"), sem("argf_ready"), sem("sel_ready"), sem("coef_ready"))
        whtr_done, whthi_ready, whtlo_ready = sem("whtr_done"), sem("whthi_ready"), sem("whtlo_ready")
        ffn_half, ffn_done, final_half, final_done = sem("ffn_half"), sem("ffn_done"), sem("final_half"), sem("final_done")

        CUTS = ((0, 384), (384, 512))

        block = ctx.enter_context(nc.Block())
        out_t = out.rearrange("(t p) d -> t p d", p=P)

        def slot16(base, off):
            return base * 4 + 16 * (off // SLOTS + 1)

        @block.sync
        def _(sp):
            sp.dma_start(par[:, :], params).then_inc(ld["par"], 16)
            sp.dma_start(trig_sb[:, 0, :], trig[:, 0, :]).then_inc(ld["trig"], 16)
            sp.dma_start(vct_sb[:, :, :], vct).then_inc(ld["vct"], 16)
            sp.dma_start(bp_sb[:, :], bp).then_inc(ld["bp"], 16)
            sp.dma_start(dft_sb[:, :, :], dft).then_inc(ld["dft"], 16)
            sp.dma_start(cos_sb[:, :], cos_s).then_inc(ld["cos"], 16)
            sp.dma_start(tw_sb[:, :], tw).then_inc(ld["tw"], 16)
            sp.dma_start(dft8_sb[:, :], dft8).then_inc(ld["d8"], 16)
            sp.dma_start(ident[:, :], ident_in).then_inc(ld["id"], 16)
            sp.wait_ge(ones_ready, 1)
            sp.dma_start(krows.rearrange("o (p c) -> (o p) c", p=P), k_zero[:, :]).then_inc(k_cleared, 16)
            sp.dma_start(w_raw[:, :, :], w_in).then_inc(ld["w"], 16)
            sp.wait_ge(ids_taken, 2)
            sp.dma_start(bw_raw[:, :], bw_in).then_inc(ld["bw"], 16)
            sp.dma_start(expert[:, :], expert_in).then_inc(ld["ex"], 16)
            sp.wait_ge(k_cleared, 16)
            for i in range(2):
                sp.wait_ge(krow_part, i + 1)
                sp.dma_start(bass.AP(tensor=krows.tensor, offset=i * KW + P - 1, ap=[[P, 2 * NB], [1, P]]),
                             k_parts[:, i, :]).then_inc(krow_stored[i], 16)
            sp.wait_ge(krow_stored[0], 16)
            def rows(part, row, a, b, base):
                return sp.dma_start(part[:, a:b], bass.AP(tensor=krows.tensor, offset=row + base + a, ap=[[1, P], [1, b - a]]))

            rows(toe_hi, 0, 0, 512, 0).then_inc(ld_toe_hi, 16)
            sp.wait_ge(krow_stored[1], 16)
            rows(toe_lo, KW, 0, 512, 0).then_inc(ld_toe_lo, 16)
            for part, row, a, b, base in ((toe_hi, 0, 512, 768, 0), (toe_lo, KW, 512, 768, 0),
                                          (dif_hi, 0, P, D, D), (dif_lo, KW, P, D, D)):
                rows(part, row, a, b, base).then_inc(ld_dif if base else ld_rest, 16)

            def store(base, off):
                sp.wait_ge(final_done, base + off + 1)
                sp.dma_start(out_t[base + off, :, :], h2[:, off % SLOTS, :]).then_inc(stored[off % SLOTS], 16)

            with sp.Fori(0, NT // SLOTS - 1) as turn:
                first = sp.snap(turn * SLOTS)
                for k in range(SLOTS):
                    store(first, k)
            for off in range(NT - SLOTS, NT - 1):
                store(0, off)
            for a, ready in ((0, final_half), (512, final_done)):
                sp.wait_ge(ready, NT)
                sp.dma_start(out_t[NT - 1, :, a:a + 512], h2[:, SLOTS - 1, a:a + 512]).then_inc(stored[SLOTS - 1], 16)
            for k in range(SLOTS):
                sp.wait_ge(stored[k], 16 * (NT // SLOTS + 1) + (16 if k == SLOTS - 1 else 0))

        @block.gpsimd
        def _(pool):
            pool.dma_start(ids_raw[:, :], ids).then_inc(ld["ids"], 16)
            for k in range(SLOTS):
                pool.sem_inc(stored[k], 16)
            G.memset(eps[:, :], EPS)
            G.memset(ones[:, :], 1.0)
            G.memset(mean_w[:, :], 1.0 / D)
            G.memset(v_mask[:, :], 0.0)
            G.memset(k_zero[:, :], 0.0).then_inc(ones_ready, 1)
            pool.wait_ge(ids_clipped, 1)

            def take_ids(base, off):
                k = off % SLOTS
                G.tensor_copy(ids_now[:, k:k + 1], ids_ok[:, bass.ds(base + off, 1)]).then_inc(ids_taken, 1)
                pool.wait_ge(ids_taken, base + off + 1)
                pool.sem_inc(pool_passed, 1)

            def gather(off):
                G.indirect_dma_start(
                    out=h0[:, off % SLOTS, :], out_offset=None, in_=table,
                    in_offset=bass.IndirectOffsetOnAxis(ap=ids_now[:, off % SLOTS:off % SLOTS + 1], axis=0),
                ).then_inc(gathered[off % SLOTS], 16)

            def centre(base, off):
                k = off % SLOTS
                pool.wait_ge(sum1_ready, base + off + 1)
                pool.sem_inc(pool_passed, 1)
                G.tensor_scalar(sc[:, k, NM1:NM1 + 1], sc[:, k, SUM1:SUM1 + 1], -1.0 / D, 1.0,
                                ALU.mult, ALU.mult).then_inc(negmean1_ready, 1)

            def scale1(base, off):
                k, n = off % SLOTS, (base + off) * 4

                def s(j):
                    return sc[:, k, j:j + 1]

                pool.wait_ge(ssq1_ready, base + off + 1)
                pool.sem_inc(pool_passed, 1)
                G.tensor_scalar(s(VE1), s(SSQ1), 1.0 / D, EPS, ALU.mult, ALU.add).then_inc(newton1, 1)
                pool.wait_ge(inv1_ready, base + off + 1)
                pool.sem_inc(pool_passed, 1)
                pool.wait_ge(newton1, n + 1)
                pool.sem_inc(pool_passed, 1)
                G.tensor_scalar(s(T0), s(VE1), s(R0), s(R0), ALU.mult, ALU.mult).then_inc(newton1, 1)
                pool.wait_ge(newton1, n + 2)
                pool.sem_inc(pool_passed, 1)
                G.tensor_scalar(s(T1), s(T0), -0.5, 1.5, ALU.mult, ALU.add).then_inc(newton1, 1)
                pool.wait_ge(newton1, n + 3)
                pool.sem_inc(pool_passed, 1)
                G.tensor_scalar(s(SC1), s(T1), s(R0), U_SCALE, ALU.mult, ALU.mult).then_inc(newton1, 1)
                pool.wait_ge(newton1, n + 4)
                pool.sem_inc(pool_passed, 1)
                G.tensor_scalar(s(NB1), s(NM1), s(SC1), 1.0, ALU.mult, ALU.mult).then_inc(scale1_ready, 1)

            for t in range(2):
                take_ids(0, t)
                gather(t)
            pool.wait_ge(v_ready, 1)
            for h in range(2):
                m = v_mask[:, h:h + 1]
                G.tensor_scalar(v_er[:, h, :], v_all[:, :], m, 1.0, ALU.mult, ALU.mult)
                G.tensor_scalar(v_ei[:, h, 0:4], v_all[:, 4:8], m, 1.0, ALU.mult, ALU.mult)
                G.tensor_scalar(v_ei[:, h, 4:8], v_all[:, 0:4], m, -1.0, ALU.mult, ALU.mult)
            for i, (a, b) in enumerate(CUTS):
                pool.wait_ge(inv_ready, i + 1)
                G.tensor_tensor(e_im[:, a:b], d_im[:, a:b], inv[:, a:b], ALU.mult).then_inc(cauchy_in[i], 1)
            for t in range(2, SLOTS):
                take_ids(0, t)
                gather(t)
            def sum_lo(base, off):
                j = off % 2
                pool.wait_ge(ushi_ready, base + off + 1)
                pool.sem_inc(pool_passed, 1)
                G.tensor_tensor(us_lo[:, j, :], u_sum[:, j, :], us_hi[:, j, :], ALU.subtract).then_inc(us_ready, 1)

            def share(base, off):
                k = off % SLOTS
                both = h0[:, k, 512:D].rearrange("p (h c) -> p h c", h=2)
                pool.wait_ge(share_out, base + off + 1)
                pool.sem_inc(pool_passed, 1)
                G.tensor_tensor(both, both, shared[:, off % 2, :].rearrange("p (o c) -> p o c", o=1).broadcast_to([P, 2, 256]),
                                ALU.add).then_inc(shared_in, 1)

            centre(0, 0)
            centre(0, 1)
            scale1(0, 0)
            scale1(0, 1)
            centre(0, 2)
            pool.wait_ge(colmax_ready, 1)
            G.partition_all_reduce(amax[:, 0:2], cmax[:, 0:2], P, RMAX).then_inc(max_ready, 1)

            def step(base, off, fetch=True, stage=True, turn=True):
                if fetch:
                    pool.wait_ge(h2_done, base + off)
                    take_ids(base, off + 3)
                    gather(off + 3)
                if stage:
                    centre(base, off + 2)
                share(base, off)
                if turn:
                    sum_lo(base, off + 1)
                if stage:
                    scale1(base, off + 2)

            sum_lo(0, 0)
            scale1(0, 2)
            step(0, 0, fetch=False, stage=False)
            with pool.Fori(0, NT // SLOTS - 1) as turn:
                first = pool.snap(turn * SLOTS)
                for k in range(SLOTS):
                    step(first, k + 1)
            step(0, NT - 3, fetch=False)
            step(0, NT - 2, fetch=False, stage=False)
            step(0, NT - 1, fetch=False, stage=False, turn=False)

        @block.scalar
        def _(act):
            act.dma_start(trig_sb[:, 1, :], trig[:, 1, :]).then_inc(ld["sin"], 16)
            act.wait_ge(ones_ready, 1)
            S.activation(warm[:, :], eps[:, :], ACT.Sqrt)
            act.wait_ge(ld["par"], 16)
            act.wait_ge(ld["trig"], 16)
            S.activation(ti[:, :], trig_sb[:, 0, :], ACT.Copy, scale=par[:, L_IM:L_IM + 1]).then_inc(cos_parts, 1)
            S.activation(d_re[:, :], trig_sb[:, 0, :], ACT.Copy, scale=par[:, L_RE:L_RE + 1]).then_inc(cos_parts, 1)
            act.wait_ge(cos_parts, 2)
            S.activation(sq_re[:, :], d_re[:, :], ACT.Square).then_inc(squares, 1)
            act.wait_ge(den_im, 1)
            S.activation(sq_im[:, :], d_im[:, :], ACT.Square).then_inc(squares, 1)
            def sum1(base, off):
                k = off % SLOTS
                act.wait_ge(gathered[k], slot16(base, off))
                S.activation(junk[:, 0, off % 2, :], h0[:, k, :], ACT.Copy, accum_out=sc[:, k, SUM1:SUM1 + 1]).then_inc(sum1_ready, 1)

            def ssq1(base, off):
                k = off % SLOTS
                act.wait_ge(negmean1_ready, base + off + 1)
                S.activation(junk[:, 1, off % 2, :], h0[:, k, :], ACT.Square, bias=sc[:, k, NM1:NM1 + 1],
                             accum_out=sc[:, k, SSQ1:SSQ1 + 1]).then_inc(ssq1_ready, 1)
                act.wait_ge(ssq1_ready, base + off + 1)
                S.activation(sc[:, k, STD1:STD1 + 1], sc[:, k, SSQ1:SSQ1 + 1], ACT.Sqrt, bias=eps[:, :],
                             scale=1.0 / D).then_inc(std1_ready, 1)

            def norm1(base, off):
                k = off % SLOTS
                act.wait_ge(scale1_ready, base + off + 1)
                S.activation(u[:, off % 2, :], h0[:, k, ::-1], ACT.Identity, bias=sc[:, k, NB1:NB1 + 1],
                             scale=sc[:, k, SC1:SC1 + 1]).then_inc(u_ready, 1)

            def hi_u(base, off):
                for h in range(2):
                    act.wait_ge(tru_done, (base + off) * 2 + h + 1)
                    S.copy(ut_hi[:, off % 2, 512 * h:512 * h + 512], tr[:, 512 * h:512 * h + 512]).then_inc(uthi_ready, 1)
                S.copy(x0_sb[:, off % 2, :], tr[:, 768:D]).then_inc(x0_ready, 1)

            def hi_z(base, off):
                for h in range(2):
                    act.wait_ge(trz_done, (base + off) * 2 + h + 1)
                    if h == 0 and (off or base is not 0):
                        act.wait_ge(ha_done, base + off)
                    S.copy(zt_hi[:, 512 * h:512 * h + 512], tr[:, 512 * h:512 * h + 512]).then_inc(zthi_ready, 1)

            def ssq2(base, off):
                k = off % SLOTS
                act.wait_ge(negmean2_ready, base + off + 1)
                S.activation(junk[:, 2, off % 2, :], h2[:, k, :], ACT.Square, bias=sc[:, k, NM2:NM2 + 1],
                             accum_out=sc[:, k, SSQ2:SSQ2 + 1]).then_inc(ssq2_ready, 1)
                act.wait_ge(ssq2_ready, base + off + 1)
                S.activation(sc[:, k, STD2:STD2 + 1], sc[:, k, SSQ2:SSQ2 + 1], ACT.Sqrt, bias=eps[:, :],
                             scale=1.0 / D).then_inc(std2_ready, 1)

            def hi_wh(base, off):
                act.wait_ge(whtr_done, base + off + 1)
                S.mul(wht_hi[:, :], ff[:, 0:P], H_SCALE).then_inc(whthi_ready, 1)

            def sum_hi(base, off):
                act.wait_ge(usum_ready, base + off + 1)
                S.copy(us_hi[:, off % 2, :], u_sum[:, off % 2, :]).then_inc(ushi_ready, 1)

            def take_shared(base, off):
                act.wait_ge(share_done, base + off + 1)
                S.activation(shared[:, off % 2, :], hx[:, SH:SH + 256], ACT.Copy, scale=scl[:, 7:8]).then_inc(share_out, 1)

            def step(base, off, one=True, two=True, stage=True, turn=True, own=True):
                if stage:
                    sum1(base, off + 2)
                if one:
                    ssq2(base, off - 1)
                if two:
                    hi_wh(base, off - 2)
                if own:
                    take_shared(base, off)
                if turn:
                    hi_u(base, off + 1)
                if stage:
                    ssq1(base, off + 2)
                if turn:
                    sum_hi(base, off + 1)
                if one:
                    hi_z(base, off - 1)
                if stage:
                    norm1(base, off + 2)

            sum1(0, 0)
            sum1(0, 1)
            ssq1(0, 0)
            ssq1(0, 1)
            norm1(0, 0)
            norm1(0, 1)
            sum1(0, 2)
            hi_u(0, 0)
            ssq1(0, 2)
            sum_hi(0, 0)
            take_shared(0, 0)
            hi_u(0, 1)
            act.wait_ge(wscale_ready, 1)
            S.activation(w_hi[:, :, :], w_raw[:, :, :], ACT.Copy, scale=scl[:, 5:6]).then_inc(whi_ready, 1)
            sum_hi(0, 1)
            S.activation(bw_hi[:, :], bw_raw[:, :], ACT.Copy, scale=scl[:, 6:7]).then_inc(whi_ready, 1)
            norm1(0, 2)
            step(0, 1, two=False)
            with act.Fori(0, NT // SLOTS - 1) as turn:
                first = act.snap(turn * SLOTS)
                for k in range(SLOTS):
                    step(first, k + 2)
            step(0, NT - 2, stage=False)
            step(0, NT - 1, stage=False, turn=False)
            step(0, NT, stage=False, turn=False, own=False)
            step(0, NT + 1, one=False, stage=False, turn=False, own=False)

        @block.vector
        def _(dve):
            steps = [0]

            def link(ins):
                steps[0] += 1
                ins.then_inc(pre_dve, 1)
                dve.wait_ge(pre_dve, steps[0])

            def c(j, n=1):
                return tiny[:, j:j + n]


            def inv1(base, off):
                k = off % SLOTS
                dve.wait_ge(std1_ready, base + off + 1)
                V.reciprocal(sc[:, k, R0:R0 + 1], sc[:, k, STD1:STD1 + 1]).then_inc(inv1_ready, 1)

            def lo_u(base, off):
                for h in range(2):
                    a = 512 * h
                    if h:
                        dve.wait_ge(x0_ready, base + off + 1)
                        V.tensor_tensor(u_sum[:, off % 2, :], tr[:, 512:768], x0_sb[:, off % 2, :], ALU.add).then_inc(usum_ready, 1)
                    else:
                        dve.wait_ge(uthi_ready, (base + off) * 2 + 1)
                    V.tensor_tensor(ut_lo[:, off % 2, a:a + 512], tr[:, a:a + 512], ut_hi[:, off % 2, a:a + 512],
                                    ALU.subtract).then_inc(utlo_ready, 1)

            T = EXP_TERMS
            f, f2 = c(2), c(3)
            dve.wait_ge(ld["par"], 16)
            link(V.tensor_scalar(c(0), par[:, LOG_STEP:LOG_STEP + 1], -87.0, 87.0, ALU.max, ALU.min))
            link(V.tensor_scalar(c(1), c(0), -LOG2E, MAGIC, ALU.mult, ALU.add))
            V.tensor_scalar(tiny_i[:, 0:1], c(1).bitcast(i32), 23, None, ALU.logical_shift_left)
            link(V.tensor_scalar(c(5), c(1), -MAGIC, None, ALU.add))
            link(V.scalar_tensor_tensor(f, c(5), -LN2_HI, c(0), ALU.mult, ALU.subtract))
            link(V.scalar_tensor_tensor(f, c(5), -LN2_LO, f, ALU.mult, ALU.add))
            V.tensor_scalar(f2, f, f, None, ALU.mult)
            for i in range(4):
                last = V.tensor_scalar(c(16 + i), f, T[2 * i + 1], T[2 * i], ALU.mult, ALU.add)
            link(last)
            V.tensor_scalar(c(20), c(17), f2, c(16), ALU.mult, ALU.add)
            V.tensor_scalar(c(21), c(19), f2, c(18), ALU.mult, ALU.add)
            link(V.tensor_scalar(c(22), f2, f2, None, ALU.mult))
            link(V.tensor_scalar(c(6), c(21), c(22), c(20), ALU.mult, ALU.add))
            link(V.tensor_tensor(c(4), c(6), tiny_i[:, 0:1].bitcast(f32), ALU.mult))
            dve.wait_ge(ld["ids"], 16)
            V.tensor_scalar(ids_ok[:, :], ids_raw[:, :], 0, VOCAB - 1, ALU.max, ALU.min).then_inc(ids_clipped, 1)
            dve.wait_ge(cos_parts, 1)
            dve.wait_ge(ld["sin"], 16)
            V.scalar_tensor_tensor(d_im[:, :], trig_sb[:, 1, :], c(4), ti[:, :], ALU.mult, ALU.subtract).then_inc(den_im, 1)
            dve.wait_ge(ones_ready, 1)
            V.memset(v_mask[0:64, 0:1], 1.0)
            V.memset(v_mask[64:128, 1:2], 1.0)
            V.tensor_copy(yv[:, 1:4:2], par[:, P_RE:P_IM + 1])
            dve.wait_ge(bvec_done, 1)
            link(V.tensor_copy(yv[:, 0:3:2], hx[:, 0:2]))
            for i, im in enumerate((C_IM, Q_IM)):
                V.tensor_scalar(c(8 + 4 * i, 2), yv[:, 2:4], par[:, im:im + 1], None, ALU.mult)
                last = V.tensor_scalar(c(10 + 4 * i, 2), yv[:, 0:2], par[:, im:im + 1], None, ALU.mult)
            link(last)
            for i, re in enumerate((C_RE, Q_RE)):
                xr = par[:, re:re + 1]
                V.scalar_tensor_tensor(v_all[:, 2 * i:2 * i + 2], yv[:, 0:2], xr, c(8 + 4 * i, 2), ALU.mult, ALU.add)
                last = V.scalar_tensor_tensor(v_all[:, 4 + 2 * i:6 + 2 * i], yv[:, 2:4], xr, c(10 + 4 * i, 2),
                                              ALU.mult, ALU.subtract)
            last.then_inc(v_ready, 1)
            dve.wait_ge(squares, 2)
            link(V.tensor_tensor(den[:, :], sq_re[:, :], sq_im[:, :], ALU.add))
            for i, (a, b) in enumerate(CUTS):
                V.reciprocal(inv[:, a:b], den[:, a:b]).then_inc(inv_ready, 1)
                dve.wait_ge(inv_ready, i + 1)
                V.scalar_tensor_tensor(e_re[:, a:b], d_re[:, a:b], -1.0, inv[:, a:b], ALU.mult, ALU.mult).then_inc(cauchy_in[i], 1)
            dve.wait_ge(cauchy_done, 1)
            link(V.tensor_copy(kap[:, :, :], y[0][:, 0:64].rearrange("p (f c) -> p c f", c=8)))
            dve.wait_ge(ld["cos"], 16)

            def pair(j):
                return kap[:, j:j + 5:4, :]

            def both(x):
                return x.rearrange("p (o f) -> p o f", o=1).broadcast_to([P, 2, NB])

            cosb = both(cos_sb[:, :])
            C01, DEN, A10, B10, NUM, SQ, U, X, INV, Q = range(10)
            V.tensor_tensor(fx[:, C01, :, :], pair(1), cosb, ALU.mult)
            link(V.tensor_tensor(fx[:, DEN, :, :], pair(3), cosb, ALU.mult))
            V.tensor_tensor(fx[:, A10, :, :], fx[:, C01, :, :], both(kap[:, 2, :]), ALU.mult)
            V.tensor_tensor(fx[:, B10, :, :], fx[:, C01, :, :], both(kap[:, 6, :]), ALU.mult)
            link(V.tensor_scalar(fx[:, DEN, 0, :], fx[:, DEN, 0, :], 1.0, None, ALU.add))
            V.tensor_tensor(fx[:, NUM, 0, :], fx[:, A10, 0, :], fx[:, B10, 1, :], ALU.subtract)
            V.tensor_tensor(fx[:, NUM, 1, :], fx[:, A10, 1, :], fx[:, B10, 0, :], ALU.add)
            link(V.tensor_tensor(fx[:, SQ, :, :], fx[:, DEN, :, :], fx[:, DEN, :, :], ALU.mult))
            V.tensor_tensor(fx[:, INV, 0, :], fx[:, SQ, 0, :], fx[:, SQ, 1, :], ALU.add)
            V.tensor_tensor(fx[:, U, :, :], fx[:, NUM, :, :], both(fx[:, DEN, 0, :]), ALU.mult)
            link(V.tensor_tensor(fx[:, Q, :, :], fx[:, NUM, :, :], both(fx[:, DEN, 1, :]), ALU.mult))
            V.reciprocal(fx[:, INV, 1, :], fx[:, INV, 0, :])
            V.tensor_tensor(fx[:, X, 0, :], fx[:, U, 0, :], fx[:, Q, 1, :], ALU.add)
            link(V.tensor_tensor(fx[:, X, 1, :], fx[:, U, 1, :], fx[:, Q, 0, :], ALU.subtract))
            link(V.tensor_tensor(fx[:, X, :, :], fx[:, X, :, :], both(fx[:, INV, 1, :]), ALU.mult))
            V.tensor_tensor(f_a[:, :, :], pair(0), fx[:, X, :, :], ALU.subtract)
            V.tensor_tensor(f_b[:, 0, :], fx[:, X, 1, :], kap[:, 4, :], ALU.subtract)
            V.tensor_tensor(f_b[:, 1, :], kap[:, 0, :], fx[:, X, 0, :], ALU.subtract).then_inc(spec_ready, 1)
            dve.wait_ge(spec_ready, 1)
            V.tensor_reduce(tiny[:, 30:31], f_a[:, :, :].rearrange("p a f -> p (a f)"), AX, ALU.add,
                            apply_absolute_value=True).then_inc(k_sum, 1)
            inv1(0, 0)
            inv1(0, 1)
            dve.wait_ge(z_done, 1)
            dve.wait_ge(ld["tw"], 16)
            link(V.tensor_tensor(zp[:, :], tw_sb[:, :], y[0][0:16, 512:512 + 2 * P], ALU.mult))
            V.tensor_tensor(zt[:, :], zp[:, 0:P], zp[:, P:2 * P], ALU.add).then_inc(zt_ready, 1)
            dve.wait_ge(k_bound, 1)
            link(V.tensor_scalar(c(34), y[1][:, 512:513], 1.0 / D, None, ALU.mult))
            V.tensor_scalar(c(35), par[:, SKIP_D:SKIP_D + 1], -1.0, par[:, SKIP_D:SKIP_D + 1], ALU.mult, ALU.max)
            link(V.tensor_scalar(c(34), c(34), 1e-30, 1.0 / TOP, ALU.max, ALU.mult))
            link(V.tensor_scalar(scl[:, 1:2], c(35), 1.0 / TOP, c(34), ALU.mult, ALU.add))
            link(V.reciprocal(scl[:, 2:3], scl[:, 1:2]))
            V.tensor_scalar(scl[:, 7:8], scl[:, 1:2], 1.0 / U_SCALE, None, ALU.mult)
            kps = y[1][0:2 * NB, 0:P]
            dve.wait_ge(k_done, 1)
            V.tensor_scalar(k_parts[:, 0, :], kps, scl[0:2 * NB, 2:3], None, ALU.mult).then_inc(krow_part, 1)
            dve.wait_ge(krow_part, 1)
            V.scalar_tensor_tensor(k_parts[:, 1, :], kps, scl[0:2 * NB, 2:3], k_parts[:, 0, :],
                                   ALU.mult, ALU.subtract).then_inc(krow_part, 1)
            dve.wait_ge(wmean_done, 1)
            dve.wait_ge(ld["w"], 16)
            link(V.tensor_copy(w_avg[:, :], ff[:, 0:W]))
            link(V.tensor_tensor(w_raw[:, :, :], w_raw[:, :, :],
                                 w_avg[:, :].rearrange("p (o w) -> p o w", o=1).broadcast_to([P, NB, W]), ALU.subtract))
            lo_u(0, 0)
            V.tensor_reduce(cmax[:, 0:1], w_raw[:, :, :].rearrange("p b w -> p (b w)"), AX, ALU.max, apply_absolute_value=True)
            dve.wait_ge(ld["bw"], 16)
            V.tensor_reduce(cmax[:, 1:2], bw_raw[:, :], AX, ALU.max, apply_absolute_value=True).then_inc(colmax_ready, 1)

            def lo_z(base, off):
                for h in range(2):
                    a = 512 * h
                    dve.wait_ge(zthi_ready, (base + off) * 2 + h + 1)
                    V.tensor_tensor(zt_lo[:, a:a + 512], tr[:, a:a + 512], zt_hi[:, a:a + 512],
                                    ALU.subtract).then_inc(ztlo_ready, 1)

            inv1(0, 2)
            dve.wait_ge(max_ready, 1)
            link(V.tensor_scalar(scl[:, 3:5], amax[:, 0:2], 1e-30, 1.0 / TOP, ALU.max, ALU.mult))
            V.reciprocal(scl[:, 5:7], scl[:, 3:5]).then_inc(wscale_ready, 1)
            link(V.tensor_tensor(scl[:, 8:9], scl[:, 3:4], scl[:, 4:5], ALU.mult))
            lo_u(0, 1)

            def residual(base, off, half):
                k, a = off % SLOTS, 512 * half
                if half:
                    dve.wait_ge(conv_done, base + off + 1)
                    dve.wait_ge(shared_in, base + off + 1)
                else:
                    dve.wait_ge(conv_half, base + off + 1)
                    dve.wait_ge(stored[k], slot16(base, off))
                last = V.scalar_tensor_tensor(h2[:, k, a:a + 512], y[off % 2][:, a:a + 512], scl[:, 7:8],
                                              h0[:, k, a:a + 512], ALU.mult, ALU.add,
                                              accum_out=sc[:, k, S2A + half:S2A + half + 1])
                if half:
                    last.then_inc(h2_done, 1)
                    dve.wait_ge(h2_done, base + off + 1)
                    V.tensor_scalar(sc[:, k, NM2:NM2 + 1], sc[:, k, S2A:S2A + 1], sc[:, k, S2B:S2B + 1], -1.0 / D,
                                    ALU.add, ALU.mult).then_inc(negmean2_ready, 1)

            def norm2(base, off):
                k, n = off % SLOTS, base + off + 1

                def s(j):
                    return sc[:, k, j:j + 1]

                dve.wait_ge(ssq2_ready, n)
                V.tensor_scalar(s(VE2), s(SSQ2), 1.0 / D, EPS, ALU.mult, ALU.add)
                dve.wait_ge(std2_ready, n)
                V.reciprocal(s(Q0), s(STD2)).then_inc(n2a, 1)
                dve.wait_ge(n2a, n)
                V.tensor_scalar(s(Q1), s(VE2), s(Q0), s(Q0), ALU.mult, ALU.mult).then_inc(n2b, 1)
                dve.wait_ge(n2b, n)
                V.tensor_scalar(s(Q2), s(Q1), -0.5, 1.5, ALU.mult, ALU.add).then_inc(n2c, 1)
                dve.wait_ge(n2c, n)
                V.tensor_scalar(s(SC2), s(Q2), s(Q0), U_SCALE, ALU.mult, ALU.mult).then_inc(n2d, 1)
                dve.wait_ge(n2d, n)
                V.tensor_scalar(z[:, off % 2, :], h2[:, k, :], s(NM2), s(SC2), ALU.add, ALU.mult).then_inc(z_ready, 1)

            def route(base, off):
                k, n = off % SLOTS, base + off + 1
                dve.wait_ge(ha_done, n)
                dve.sem_inc(dve_passed, 1)
                V.max(top8[:, :], hx[:, 0:E]).then_inc(top_ready, 1)
                dve.wait_ge(top_ready, n)
                dve.sem_inc(dve_passed, 1)
                V.max_index(arg8[:, :], top8[:, :], hx[:, 0:E]).then_inc(arg_ready, 1)
                dve.wait_ge(arg_ready, n)
                V.tensor_copy(argf[:, :], arg8[:, 0:1]).then_inc(argf_ready, 1)
                dve.wait_ge(argf_ready, n)
                V.scalar_tensor_tensor(sel[:, :], expert[:, :], argf[:, :], hx[:, E:W],
                                       ALU.is_equal, ALU.mult).then_inc(sel_ready, 1)
                V.tensor_scalar(coef[:, k:k + 1], top8[:, 0:1], scl[:, 3:4], scl[:, 8:9],
                                ALU.mult, ALU.mult).then_inc(coef_ready, 1)

            def lo_wh(base, off):
                dve.wait_ge(whthi_ready, base + off + 1)
                V.scalar_tensor_tensor(wht_lo[:, :], ff[:, 0:P], H_SCALE, wht_hi[:, :],
                                       ALU.mult, ALU.subtract).then_inc(whtlo_ready, 1)

            def final(base, off, half, bank=ff):
                k, n, a = off % SLOTS, base + off + 1, 512 * half
                dve.wait_ge(ffn_done if half else ffn_half, n)
                if not half:
                    dve.wait_ge(coef_ready, n)
                V.scalar_tensor_tensor(h2[:, k, a:a + 512], bank[:, 0:512], coef[:, k:k + 1], h2[:, k, a:a + 512],
                                       ALU.mult, ALU.add).then_inc(final_done if half else final_half, 1)

            def step(base, off, one=True, two=True, stage=True, turn=True, own=True):
                if two:
                    route(base, off - 2)
                if one:
                    norm2(base, off - 1)
                if two:
                    lo_wh(base, off - 2)
                if turn:
                    lo_u(base, off + 1)
                if stage:
                    inv1(base, off + 2)
                if own:
                    residual(base, off, 0)
                if two and own:
                    final(base, off - 2, 0)
                if one:
                    lo_z(base, off - 1)
                if two and not own:
                    final(base, off - 2, 0)
                if two:
                    final(base, off - 2, 1, ff if own else y[0])
                if own:
                    residual(base, off, 1)

            dve.wait_ge(ld["ex"], 16)
            residual(0, 0, 0)
            residual(0, 0, 1)
            dve.wait_ge(whi_ready, 1)
            V.scalar_tensor_tensor(w_lo[:, :, :], w_raw[:, :, :], scl[:, 5:6], w_hi[:, :, :], ALU.mult, ALU.subtract)
            dve.wait_ge(whi_ready, 2)
            V.scalar_tensor_tensor(bw_lo[:, :], bw_raw[:, :], scl[:, 6:7], bw_hi[:, :], ALU.mult, ALU.subtract).then_inc(weights_ready, 1)
            step(0, 1, two=False)
            with dve.Fori(0, NT // SLOTS - 1) as turn:
                first = dve.snap(turn * SLOTS)
                for k in range(SLOTS):
                    step(first, k + 2)
            step(0, NT - 2, stage=False)
            step(0, NT - 1, stage=False, turn=False)
            step(0, NT, stage=False, turn=False, own=False)
            step(0, NT + 1, one=False, stage=False, turn=False, own=False)

        @block.tensor
        def _(pe):
            def transposes(base, off, rows, ready, free, freed, done):
                pe.wait_ge(ready, base + off + 1)
                for b in range(NB):
                    if free is not None and b % 4 == 0:
                        pe.wait_ge(free, freed + b // 4)
                    last = PE.transpose(tr[:, b * P:(b + 1) * P], rows[:, off % 2, b * P:(b + 1) * P], ident[:, :])
                    if b % 4 == 3:
                        last.then_inc(done, 1)

            pe.wait_ge(ld["vct"], 16)
            pe.wait_ge(ld["bp"], 16)
            for c in range(2):
                last = PE.matmul(hx[:, c:c + 1], vct_sb[:, c, :], bp_sb[:, :], start=True, stop=True)
            last.then_inc(bvec_done, 1)
            pe.wait_ge(ld["w"], 16)
            pe.wait_ge(ones_ready, 1)
            for b in range(NB):
                last = PE.matmul(ff[:, 0:W], mean_w[:, :], w_raw[:, b, :], start=(b == 0), stop=(b == NB - 1))
            last.then_inc(wmean_done, 1)
            pe.wait_ge(cauchy_in[0], 2)
            for g in range(4):
                if P * g == CUTS[1][0]:
                    pe.wait_ge(cauchy_in[1], 2)
                o = y[0][:, 16 * g:16 * g + 16]
                PE.matmul(o, e_re[:, P * g:P * g + P], v_er[:, :, :].rearrange("p h c -> p (h c)"), start=True, stop=False)
                last = PE.matmul(o, e_im[:, P * g:P * g + P], v_ei[:, :, :].rearrange("p h c -> p (h c)"), start=False, stop=True)
            last.then_inc(cauchy_done, 1)
            pe.wait_ge(spec_ready, 1)
            pe.wait_ge(ld["dft"], 16)
            o = y[0][0:16, 512:512 + 2 * P]
            PE.matmul(o, f_a[:, :, :].rearrange("p a f -> p (a f)"), dft_sb[:, 0, :], start=True, stop=False)
            PE.matmul(o, f_b[:, :, :].rearrange("p a f -> p (a f)"), dft_sb[:, 1, :], start=False, stop=True).then_inc(z_done, 1)
            pe.wait_ge(ld["id"], 16)
            pe.wait_ge(k_sum, 1)
            PE.matmul(y[1][:, 512:513], ones[:, :], tiny[:, 30:31], start=True, stop=True).then_inc(k_bound, 1)
            pe.wait_ge(ld["d8"], 16)
            pe.wait_ge(zt_ready, 1)
            PE.matmul(y[1][0:2 * NB, 0:P], dft8_sb[:, 0:2 * NB], zt[:, :], start=True, stop=True, skip_group_check=True)
            PE.matmul(y[1][0:2 * NB, 0:1], dft8_sb[0:1, 2 * NB:4 * NB], par[0:1, SKIP_D:SKIP_D + 1], start=False, stop=True,
                      skip_group_check=True).then_inc(k_done, 1)
            pe.wait_ge(ld["id"], 16)

            def product(o, x_hi, x_lo, t_hi, t_lo, first=False, stop=False, lo_ready=None):
                PE.matmul(o, x_hi, t_hi, start=first, stop=False, skip_group_check=True)
                PE.matmul(o, x_lo, t_hi, start=False, stop=False, skip_group_check=True)
                if lo_ready is not None:
                    pe.wait_ge(lo_ready, 16)
                return PE.matmul(o, x_hi, t_lo, start=False, stop=stop, skip_group_check=True)

            def block(off, jb):
                x = D - (jb + 1) * P
                return ut_hi[:, off % 2, x:x + P], ut_lo[:, off % 2, x:x + P]

            def near(off, jb):
                end = 512 if jb < 4 else D
                n = end - jb * P
                return product(y[off % 2][:, jb * P:end], *block(off, jb), toe_hi[:, 0:n], toe_lo[:, 0:n], first=(jb % 4 == 0),
                               lo_ready=ld_toe_lo if off == 0 and jb == 0 else None)

            def far(off, jb):
                a = 768 if jb < 2 else 512
                c = a - jb * P
                return product(y[off % 2][:, a:a + 256], *block(off, jb), dif_hi[:, c:c + 256], dif_lo[:, c:c + 256])

            def share(base, off):
                pe.wait_ge(us_ready, base + off + 1)
                if off == 0:
                    pe.wait_ge(ld_rest, 32)
                if off or base is not 0:
                    pe.wait_ge(share_out, base + off)
                for i in range(2):
                    x, c = P * (1 - i), 512 - P * i
                    last = product(hx[:, SH:SH + 256], us_hi[:, off % 2, x:x + P], us_lo[:, off % 2, x:x + P],
                                   toe_hi[:, c:c + 256], toe_lo[:, c:c + 256], first=(i == 0), stop=(i == 1))
                last.then_inc(share_done, 1)

            def experts_in(base, off, shared):
                if off == 0:
                    pe.wait_ge(weights_ready, 1)
                if shared:
                    pe.wait_ge(share_out, base + off + 2)
                for b in range(NB):
                    if b % 4 == 0:
                        pe.wait_ge(ztlo_ready, (base + off) * 2 + b // 4 + 1)
                    for i, (part, w) in enumerate(((zt_hi, w_hi), (zt_hi, w_lo), (zt_lo, w_hi))):
                        last = PE.matmul(hx[:, 0:W], part[:, b * P:(b + 1) * P], w[:, b, :],
                                         start=(b == 0 and i == 0), stop=(b == NB - 1 and i == 2))
                last.then_inc(ha_done, 1)

            def transpose_wh(base, off):
                pe.wait_ge(sel_ready, base + off + 1)
                if off or base is not 0:
                    pe.wait_ge(final_done, base + off)
                PE.transpose(ff[:, 0:P], sel[:, :], ident[:, :]).then_inc(whtr_done, 1)

            def experts_out(base, off, half, bank=ff):
                a = 512 * half
                if half and bank is ff:
                    pe.wait_ge(final_half, base + off + 1)
                elif not half:
                    pe.wait_ge(whtlo_ready, base + off + 1)
                for i, (part, bw) in enumerate(((wht_hi, bw_hi), (wht_hi, bw_lo), (wht_lo, bw_hi))):
                    last = PE.matmul(bank[:, 0:512], part[:, :], bw[:, a:a + 512], start=(i == 0), stop=(i == 2))
                last.then_inc(ffn_done if half else ffn_half, 1)

            def step(base, off, one=True, two=True, turn=True, own=True):
                if own:
                    pe.wait_ge(utlo_ready, (base + off) * 2 + 2)
                    if off > 1 or base is not 0:
                        pe.wait_ge(h2_done, base + (off - 1))
                    near(off, 0)
                    near(off, 1)
                    near(off, 2)
                if own:
                    near(off, 3).then_inc(conv_half, 1)
                if two:
                    transpose_wh(base, off - 2)
                if own:
                    share(base, off)
                if turn:
                    if off == 0:
                        transposes(base, off + 1, u, u_ready, utlo_ready, 1, tru_done)
                    elif off == 1 and base is 0:
                        transposes(base, off + 1, u, u_ready, utlo_ready, 3, tru_done)
                    else:
                        transposes(base, off + 1, u, u_ready, ztlo_ready, (base + off - 2) * 2 + 1, tru_done)
                if own:
                    near(off, 4)
                    if off == 0:
                        pe.wait_ge(ld_dif, 32)
                    for jb in range(4):
                        far(off, jb)
                if two and (own or not one):
                    experts_out(base, off - 2, 0)
                if one and off > 1:
                    if turn:
                        transposes(base, off - 1, z, z_ready, utlo_ready, (base + off + 1) * 2 + 1, trz_done)
                    else:
                        transposes(base, off - 1, z, z_ready, ztlo_ready, (base + off - 2) * 2 + 1, trz_done)
                if own:
                    near(off, 5)
                    near(off, 6)
                if two and one and not own:
                    experts_out(base, off - 2, 0)
                if two:
                    experts_out(base, off - 2, 1, ff if own else y[0])
                if own:
                    near(off, 7).then_inc(conv_done, 1)
                if off == 1:
                    transposes(base, 0, z, z_ready, utlo_ready, 5, trz_done)
                if one:
                    experts_in(base, off - 1, own)

            transposes(0, 0, u, u_ready, None, 0, tru_done)
            pe.wait_ge(ld_toe_hi, 16)
            step(0, 0, one=False, two=False)
            step(0, 1, two=False)
            with pe.Fori(0, NT // SLOTS - 1) as turn:
                first = pe.snap(turn * SLOTS)
                for k in range(SLOTS):
                    step(first, k + 2)
            step(0, NT - 2)
            step(0, NT - 1, turn=False)
            step(0, NT, turn=False, own=False)
            step(0, NT + 1, one=False, turn=False, own=False)


def constants():
    lp = np.arange(P, dtype=np.float64)
    res = np.array([4 * h + g for g in range(4) for h in range(2)], dtype=np.float64)
    half = np.arange(P) // NS
    bins = 8 * lp[None, None, :] + 4 * half[:, None, None] + np.arange(4)[None, :, None]
    phi = np.pi * bins / D
    cosphi = np.where(bins == D // 2, 0.0, np.cos(phi))
    trig = np.stack([cosphi.reshape(P, 512), np.sin(phi).reshape(P, 512)], 1)
    b2 = 8 * lp[:, None] + res[None, :]
    cos_s = np.where(b2 == D // 2, 0.0, np.cos(np.pi * b2 / D))
    t1 = np.arange(P)
    ang = np.pi * ((lp[:, None].astype(np.int64) * (2 * t1[None, :] + 1)) % 256) / 128
    c, s = np.cos(ang), np.sin(ang)
    dft = np.stack([np.concatenate([c, -s], 1), np.concatenate([s, c], 1)], 1)
    th = np.pi * res[:, None] * (2 * t1[None, :] + 1) / D
    tw = np.tile(np.concatenate([np.cos(th), np.sin(th)], 1), (2, 1))
    th = np.pi * res[:, None] * np.arange(NB)[None, :] / 4
    dft8 = np.zeros((16, 4 * NB))
    k = np.concatenate([np.cos(th), -np.sin(th)], 0) / D
    dft8[:, :NB] = k
    dft8[:, NB:NB + 4] = k[:, :4] - k[:, 2:6]
    dft8[:, NB + 4:2 * NB] = k[:, 4:] - k[:, 2:6]
    dft8[0, 2 * NB] = 1.0
    expert = np.broadcast_to(np.arange(E * R) // R, (P, E * R))
    f = np.float32
    return trig.astype(f), cos_s.astype(f), dft.astype(f), tw.astype(f), dft8.astype(f), np.eye(P, dtype=f), expert.astype(f)


def kernel(x, L0_tok_orig_emb_w, L0_tok_new_emb, L0_attn_Lambda_ri, L0_attn_p_ri, L0_attn_q_ri, L0_attn_Vc_ri,
           L0_attn_Ct_ri, L0_attn_Bp, L0_attn_D, L0_attn_log_step, L0_ffn_route_w, L0_ffn_A, L0_ffn_Bw):
    import concourse.bacc as bacc
    from concourse.bass_utils import run_bass_kernel_spmd

    def a(v):
        return np.asarray(v)

    trig, cos_s, dft, tw, dft8, ident, expert = constants()
    lam, p, q, ct = (a(v).reshape(NS, 2) for v in (L0_attn_Lambda_ri, L0_attn_p_ri, L0_attn_q_ri, L0_attn_Ct_ri))
    cols = np.concatenate([lam, p, q, ct], 1)
    ends = np.broadcast_to(np.stack([a(L0_attn_log_step)[0], a(L0_attn_D)[0]]), (P, 2))
    params = np.concatenate([np.concatenate([cols, cols], 0), ends], 1)
    vct = a(L0_attn_Vc_ri).transpose(1, 2, 0)
    w = np.concatenate([a(L0_ffn_route_w).T, a(L0_ffn_A).reshape(E * R, D).T], 1)
    arrays = {
        "ids": a(x).reshape(NT, P).T,
        "table": np.concatenate([a(L0_tok_orig_emb_w), a(L0_tok_new_emb)], 0),
        "params": params,
        "vct": np.concatenate([vct, vct], 2),
        "bp": a(L0_attn_Bp),
        "w": w.reshape(NB, P, W).transpose(1, 0, 2),
        "bw": a(L0_ffn_Bw).transpose(0, 2, 1).reshape(E * R, D),
        "trig": trig, "cos_s": cos_s, "dft": dft, "tw": tw, "dft8": dft8, "ident": ident, "expert": expert,
    }
    arrays = {f"in_{n}": np.ascontiguousarray(v) for n, v in arrays.items()}
    nc = bacc.Bacc("TRN2", target_bir_lowering=False, num_devices=1)
    args = [nc.dram_tensor(n, v.shape, mybir.dt.from_np(v.dtype), kind="ExternalInput").ap() for n, v in arrays.items()]
    krows = nc.dram_tensor("krows", (1, 2 * (P + 2 * D)), mybir.dt.float16, kind="Internal").ap()
    out = nc.dram_tensor("out_rows", (TOK, D), mybir.dt.float32, kind="ExternalOutput").ap()
    build(nc, *args, krows, out)
    r = run_bass_kernel_spmd(nc, [arrays], core_ids=[0])
    return r.results[0]["out_rows"].reshape(8, 512, D)
```
